# Optimizing a Trainium2 kernel written in Bass

```python
import numpy as np
import jax
import jax.numpy as jnp

def _softmax(x, axis=-1):
    return jax.nn.softmax(x, axis=axis)
def _gelu(x):
    return jax.nn.gelu(x, approximate=True)
def _silu(x):
    return jax.nn.silu(x)
def _sigmoid(x):
    return jax.nn.sigmoid(x)
def _layernorm(x, axis=-1, eps=1e-5):
    m = jnp.mean(x, axis=axis, keepdims=True)
    v = jnp.var(x, axis=axis, keepdims=True)
    return (x - m) / jnp.sqrt(v + eps)
def _scatter_add(tgt, idx, src, axis=0):
    return tgt.at[idx].add(src)
def _segment_sum(src, seg, n):
    return jax.ops.segment_sum(src, seg, n)

kernel_name = 'mk_adj_ffn_d2_adj_256_032f1b'

def setup_inputs(seed: int = 0):
    np.random.seed(seed)
    _w = jnp.asarray
    def _rec_inputs():
        import jax
        import jax.numpy as jnp
        _gk = jax.random.key(seed)
        x = -0.0002928 + 1 * jax.random.normal(jax.random.fold_in(_gk, 1), (128, 64, 256), jnp.float32)
        _w = (1.0 + jnp.arange(64, dtype=jnp.float32)) ** -0.5
        _w = _w / _w.mean()
        _pij = jnp.clip(0.125 * _w[:, None] * _w[None, :], 0.0, 1.0)
        _a = jax.random.uniform(jax.random.fold_in(_gk, 2), (128, 64, 64)) < _pij
        adj = _a.astype(jnp.int32)
        return x, adj
    x, adj = _rec_inputs()
    def _L0_gnn_setup():
        import jax, jax.numpy as jnp
        import numpy as np
        NEG_BIG = -9000000000000000.0
        key = jax.random.key(seed)
        k_h, k_adj, k_W, k_a = jax.random.split(key, 4)
        B, N, F_in, F_out = (8, 2048, 256, 256)
        h = jax.random.normal(k_h, (B, N, F_in), dtype=jnp.float32)
        adj = jax.random.randint(k_adj, (B, N, N), 0, 2, dtype=jnp.int32)
        gain = 1.414
        lim_W = gain * np.sqrt(6.0 / (F_in + F_out))
        W = jax.random.uniform(k_W, (F_in, F_out), dtype=jnp.float32, minval=-lim_W, maxval=lim_W)
        lim_a = gain * np.sqrt(6.0 / (2 * F_out + 1))
        a = jax.random.uniform(k_a, (2 * F_out, 1), dtype=jnp.float32, minval=-lim_a, maxval=lim_a)
        return {'h': h, 'adj': adj, 'W': W, 'a': a}
    _L0_gnn_all = _L0_gnn_setup()
    _L0_gnn_in = {k: v for k, v in _L0_gnn_all.items() if k in ('W', 'a', )}
    del _L0_gnn_all

    def _L0_ffn_setup():
        import jax, jax.numpy as jnp
        import numpy as np
        NUM_EXPERTS = 8
        TOP_K = 2
        B, S, D = (8, 8192, 256)

        def _moe(tokens, router_w, w1, b1, w2, b2):
            N = tokens.shape[0]
            E = router_w.shape[0]
            logits = tokens.astype(jnp.float32) @ router_w.astype(jnp.float32).T
            probs = jax.nn.softmax(logits, axis=-1)
            rw, re = jax.lax.top_k(probs, TOP_K)
            if TOP_K > 1:
                rw = rw / jnp.maximum(rw.sum(-1, keepdims=True), 1e-12)
            rw = rw.astype(tokens.dtype)
            combine = jnp.zeros((N, E), tokens.dtype).at[jnp.arange(N)[:, None], re].set(rw)
            out = tokens
            for e in range(E):
                h = jax.nn.gelu(tokens @ w1[e] + b1[e], approximate=False)
                y = h @ w2[e] + b2[e]
                out = out + combine[:, e:e + 1] * y
            return out
        key = jax.random.key(seed)
        ks = jax.random.split(key, 4)
        scale = 1.0 / np.sqrt(D).astype(np.float32)
        return {'input_embeddings': jax.random.normal(ks[0], (B, S, D), jnp.float32), 'router_w': jax.random.normal(ks[1], (NUM_EXPERTS, D), jnp.float32) * scale, 'w1': jax.random.normal(ks[2], (NUM_EXPERTS, D, D), jnp.float32) * scale, 'b1': jnp.zeros((NUM_EXPERTS, D), jnp.float32), 'w2': jax.random.normal(ks[3], (NUM_EXPERTS, D, D), jnp.float32) * scale, 'b2': jnp.zeros((NUM_EXPERTS, D), jnp.float32)}
    _L0_ffn_all = _L0_ffn_setup()
    _L0_ffn_in = {k: v for k, v in _L0_ffn_all.items() if k in ('router_w', 'w1', 'b1', 'w2', 'b2', )}
    del _L0_ffn_all

    def _L1_gnn_setup():
        import jax, jax.numpy as jnp
        import numpy as np
        ALPHA = 0.2
        NEG_BIG = -9000000000000000.0
        key = jax.random.key(seed)
        k1, k2, k3, k4 = jax.random.split(key, 4)
        B, N, F_in, F_out = (8, 2048, 256, 256)
        x = jax.random.normal(k1, (B, N, F_in), dtype=jnp.float32)
        adj = jax.random.randint(k2, (B, N, N), 0, 2, dtype=jnp.int32)
        limW = float(np.sqrt(6.0 / (F_in + F_out)))
        W = jax.random.uniform(k3, (F_in, F_out), minval=-limW, maxval=limW, dtype=jnp.float32)
        lima = float(np.sqrt(6.0 / (2 * F_out + 1)))
        a = jax.random.uniform(k4, (2 * F_out, 1), minval=-lima, maxval=lima, dtype=jnp.float32)
        return {'x': x, 'adj': adj, 'W': W, 'a': a}
    _L1_gnn_all = _L1_gnn_setup()
    _L1_gnn_in = {k: v for k, v in _L1_gnn_all.items() if k in ('W', 'a', )}
    del _L1_gnn_all

    def _L1_ffn_setup():
        import jax, jax.numpy as jnp
        import numpy as np
        D_MODEL = 256
        EXPERT_DIM = 512
        NUM_EXPERTS = 8
        TOP_K = 2
        SEQ_LEN = 2048
        BATCH = 2
        key = jax.random.key(seed)
        ks = jax.random.split(key, 8)
        s = 0.02
        x = jax.random.normal(ks[0], (SEQ_LEN, BATCH, D_MODEL), dtype=jnp.float32)
        Wg = jax.random.normal(ks[1], (D_MODEL, NUM_EXPERTS), dtype=jnp.float32) * s
        bg = jax.random.normal(ks[2], (NUM_EXPERTS,), dtype=jnp.float32) * s
        bias = jnp.zeros((NUM_EXPERTS,), dtype=jnp.float32)
        W1 = jax.random.normal(ks[3], (NUM_EXPERTS, D_MODEL, EXPERT_DIM), dtype=jnp.float32) * s
        b1 = jax.random.normal(ks[4], (NUM_EXPERTS, EXPERT_DIM), dtype=jnp.float32) * s
        W2 = jax.random.normal(ks[5], (NUM_EXPERTS, EXPERT_DIM, D_MODEL), dtype=jnp.float32) * s
        b2 = jax.random.normal(ks[6], (NUM_EXPERTS, D_MODEL), dtype=jnp.float32) * s
        return {'x': x, 'Wg': Wg, 'bg': bg, 'bias': bias, 'W1': W1, 'b1': b1, 'W2': W2, 'b2': b2}
    _L1_ffn_all = _L1_ffn_setup()
    _L1_ffn_in = {k: v for k, v in _L1_ffn_all.items() if k in ('Wg', 'bg', 'bias', 'W1', 'b1', 'W2', 'b2', )}
    del _L1_ffn_all

    return {
        "x": x,
        "adj": adj,
        "L0_gnn_W": _L0_gnn_in["W"],
        "L0_gnn_a": _L0_gnn_in["a"],
        "L0_ffn_router_w": _L0_ffn_in["router_w"],
        "L0_ffn_w1": _L0_ffn_in["w1"],
        "L0_ffn_b1": _L0_ffn_in["b1"],
        "L0_ffn_w2": _L0_ffn_in["w2"],
        "L0_ffn_b2": _L0_ffn_in["b2"],
        "L1_gnn_W": _L1_gnn_in["W"],
        "L1_gnn_a": _L1_gnn_in["a"],
        "L1_ffn_Wg": _L1_ffn_in["Wg"],
        "L1_ffn_bg": _L1_ffn_in["bg"],
        "L1_ffn_bias": _L1_ffn_in["bias"],
        "L1_ffn_W1": _L1_ffn_in["W1"],
        "L1_ffn_b1": _L1_ffn_in["b1"],
        "L1_ffn_W2": _L1_ffn_in["W2"],
        "L1_ffn_b2": _L1_ffn_in["b2"],
    }

def reference(x, adj, L0_gnn_W, L0_gnn_a, L0_ffn_router_w, L0_ffn_w1, L0_ffn_b1, L0_ffn_w2, L0_ffn_b2, L1_gnn_W, L1_gnn_a, L1_ffn_Wg, L1_ffn_bg, L1_ffn_bias, L1_ffn_W1, L1_ffn_b1, L1_ffn_W2, L1_ffn_b2):
    import jax
    import jax.numpy as jnp
    def _L0_gnn_ref(h, adj, W, a):
        import jax, jax.numpy as jnp
        import numpy as np
        NEG_BIG = -9000000000000000.0
        F_out = W.shape[1]
        Wh = jnp.matmul(h, W)
        a1 = a[:F_out, 0]
        a2 = a[F_out:, 0]
        e = (Wh @ a1)[:, :, None] + (Wh @ a2)[:, None, :]
        masked = jnp.where(adj > 0, e, jnp.float32(NEG_BIG))
        attention = jax.nn.softmax(masked, axis=-1)
        h_prime = jnp.matmul(attention, Wh)
        return jax.nn.elu(h_prime)

    def _L0_ffn_ref(input_embeddings, router_w, w1, b1, w2, b2):
        import jax, jax.numpy as jnp
        import numpy as np
        NUM_EXPERTS = 8
        TOP_K = 2
        B, S, D = (8, 8192, 256)

        def _moe(tokens, router_w, w1, b1, w2, b2):
            N = tokens.shape[0]
            E = router_w.shape[0]
            logits = tokens.astype(jnp.float32) @ router_w.astype(jnp.float32).T
            probs = jax.nn.softmax(logits, axis=-1)
            rw, re = jax.lax.top_k(probs, TOP_K)
            if TOP_K > 1:
                rw = rw / jnp.maximum(rw.sum(-1, keepdims=True), 1e-12)
            rw = rw.astype(tokens.dtype)
            combine = jnp.zeros((N, E), tokens.dtype).at[jnp.arange(N)[:, None], re].set(rw)
            out = tokens
            for e in range(E):
                h = jax.nn.gelu(tokens @ w1[e] + b1[e], approximate=False)
                y = h @ w2[e] + b2[e]
                out = out + combine[:, e:e + 1] * y
            return out
        b, s, d = input_embeddings.shape
        tokens = input_embeddings.reshape(b * s, d)
        return _moe(tokens, router_w, w1, b1, w2, b2).reshape(b, s, d)

    def _L1_gnn_ref(x, adj, W, a):
        import jax, jax.numpy as jnp
        import numpy as np
        ALPHA = 0.2
        NEG_BIG = -9000000000000000.0
        F_out = W.shape[1]
        Wh = jnp.einsum('bnf,fo->bno', x, W)
        a1, a2 = (a[:F_out, 0], a[F_out:, 0])
        e = (Wh @ a1)[:, :, None] + (Wh @ a2)[:, None, :]
        e = jnp.where(e > 0, e, ALPHA * e)
        attention = jnp.where(adj > 0, e, NEG_BIG)
        attention = jax.nn.softmax(attention, axis=-1)
        h_prime = jnp.einsum('bij,bjo->bio', attention, Wh)
        return jax.nn.elu(h_prime)

    def _L1_ffn_ref(x, Wg, bg, bias, W1, b1, W2, b2):
        import jax, jax.numpy as jnp
        import numpy as np
        D_MODEL = 256
        EXPERT_DIM = 512
        NUM_EXPERTS = 8
        TOP_K = 2
        SEQ_LEN = 2048
        BATCH = 2
        x_flat = x.reshape(-1, D_MODEL)
        gate_logits = x_flat @ Wg + bg + bias
        topk_vals, topk_idx = jax.lax.top_k(gate_logits, TOP_K)
        topk_w = jax.nn.softmax(topk_vals, axis=-1)
        combine = (jax.nn.one_hot(topk_idx, NUM_EXPERTS, dtype=x.dtype) * topk_w[..., None]).sum(axis=1)
        h = jax.nn.relu(jnp.einsum('td,edh->teh', x_flat, W1) + b1)
        y = jnp.einsum('teh,ehd->ted', h, W2) + b2
        out = jnp.einsum('ted,te->td', y, combine)
        return out.reshape(x.shape)

    x = x + _L0_gnn_ref(_layernorm(x, axis=-1), adj, L0_gnn_W, L0_gnn_a)
    x = x + _L0_ffn_ref(_layernorm(x, axis=-1), L0_ffn_router_w, L0_ffn_w1, L0_ffn_b1, L0_ffn_w2, L0_ffn_b2)
    x = x + _L1_gnn_ref(_layernorm(x, axis=-1), adj, L1_gnn_W, L1_gnn_a)
    x = x + _L1_ffn_ref(_layernorm(x, axis=-1), L1_ffn_Wg, L1_ffn_bg, L1_ffn_bias, L1_ffn_W1, L1_ffn_b1, L1_ffn_W2, L1_ffn_b2)
    return x


_drawn_inputs = setup_inputs


def setup_inputs(seed=0):
    import zlib

    import numpy as np

    out = dict(_drawn_inputs(seed))
    spreads = {'L0_ffn_b1': (0.0, 0.377), 'L0_ffn_b2': (0.0, 0.1), 'L1_ffn_bias': (0.0, 0.63)}
    factors = {'L1_ffn_bg': 8.0, 'L1_ffn_b1': 33.008, 'L1_ffn_b2': 8.0}
    for name, (base, spread) in spreads.items():
        noise = np.random.default_rng([zlib.crc32(name.encode()), seed]).standard_normal(out[name].shape)
        drawn = base * np.exp(spread * noise) if base else spread * noise
        out[name] = jnp.asarray(drawn.astype(out[name].dtype))
    for name, factor in factors.items():
        out[name] = (out[name] * factor).astype(out[name].dtype)
    return out
```

```python
import concourse.bass as bass
from concourse import mybir
from contextlib import ExitStack

F32 = mybir.dt.float32
F16 = mybir.dt.float16
I32 = mybir.dt.int32
U32 = mybir.dt.uint32
ALU = mybir.AluOpType
ACT = mybir.ActivationFunctionType
AX = mybir.AxisListType

P = 128
GRAPHS = 128
NODES = 64
D = 256
KC = D // P
TOKENS = GRAPHS * NODES
TILES = TOKENS // P
GT = 8
GROUPS = TILES // GT
E = 8
TOPK = 2
SLOTS = TOKENS * TOPK // P + E
SU = 4
HID = (256, 512)
NEG_BIG = -9000000000000000.0
EPS = 1e-5
LEAK = 0.2
WSCALE = 64.0
AHEAD = 16


def at(n):
    return n + AHEAD


def build(nc, x_in, adj, W_gnn, a_gnn, router, gate_b, gate_bias, w1, b1, w2, b2, out):
    ctx = ExitStack()
    with ctx:
        def sb(name, shape, dt=F32):
            return ctx.enter_context(nc.sbuf_tensor(name, shape, dt))

        def sem(name):
            return ctx.enter_context(nc.semaphore(name))

        def sem2(name):
            return [ctx.enter_context(nc.semaphore(f"{name}_{L}")) for L in range(2)]

        table = [nc.dram_tensor(f"split_tokens_{L}", (TOKENS, 2 * D), F16, kind="Internal").ap() for L in range(2)]
        ydram = [nc.dram_tensor(f"slot_outputs_{L}", (SLOTS * P, D), F32, kind="Internal").ap() for L in range(2)]

        X = sb("X", [P, TILES * D])
        WREG = sb("WREG", [P, E * (4 * HID[1] + 4 * HID[1])], F16)
        ident = sb("ident", [P, P])
        ident16 = sb("ident16", [P, P], F16)
        before16 = sb("before16", [P, P], F16)
        ones16 = sb("ones16", [P, P], F16)
        same_graph = sb("same_graph", [P, P])
        stacked_id = sb("stacked_id", [P, NODES])
        iota_p = sb("iota_p", [P, P])
        iota_s = sb("iota_s", [P, SLOTS])
        token_id = sb("token_id", [P, TILES])
        rank8 = sb("rank8", [P, E])
        eps_col = sb("eps_col", [P, 1])
        wg_sb = sb("wg_sb", [P, 2 * KC * D])
        abc = sb("abc", [P, 4 * P])
        a_cols = sb("a_cols", [P, 2 * 4])
        wgT = sb("wgT", [P, KC * D])
        rt_sb = sb("rt_sb", [P, 2 * KC * E])
        rt_rows = sb("rt_rows", [E, D])
        u_bc = sb("u_bc", [P, 2 * D])
        u_sum = sb("u_sum", [P, 2])
        gb_bc = sb("gb_bc", [P, 2 * E])
        b2_low64 = sb("b2_low64", [P, 1])
        b2_sign = sb("b2_sign", [P, 1])
        b1T = sb("b1T", [P, E * (HID[0] + HID[1]) // P])
        b2_pair = sb("b2_pair", [P, E * D], F16)
        b2_pick = sb("b2_pick", [P, 2 * P], F16)
        stats = sb("stats", [P, TILES * 6])
        cols = sb("cols", [P, 24 * TILES])
        names = ["mean", "rstd", "nmr", "s1", "s2", "dot1", "dot2", "ta", "tb", "tc", "w1", "w2",
                 "m1", "m2", "rk", "lo0", "hi0", "lo1", "hi1", "rs2", "nm2", "var", "sd", "td"]
        col = {n: cols[:, k * TILES:(k + 1) * TILES] for k, n in enumerate(names)}

        pos_i = [sb(f"pos_i{k}", [P, TILES], I32) for k in range(TOPK)]
        tmp_i = sb("tmp_i", [P, TILES], I32)
        slot_token = sb("slot_token", [P, SLOTS], U32)
        slot_expert = sb("slot_expert", [1, SLOTS], I32)
        ex = sb("ex", [P, 12 * 9])
        ex_i = sb("ex_i", [P, 2 * E], I32)
        index_now = sb("index_now", [P, 8], U32)
        rinv = sb("rinv", [P, 2 * GT])

        arena = sb("arena", [P, 9728])
        used = [0]

        def carve(n, start=None):
            if start is not None:
                used[0] = start
            a = arena[:, used[0]:used[0] + n]
            used[0] += n
            assert used[0] <= 9728
            return a

        adj_sb = carve(512, 0).bitcast(I32)
        neg = carve(512)
        diag = carve(512)
        scores = carve(512)
        probs = carve(GT * P)
        probsT = carve(GT * P)
        xn = carve(GT * D)
        gT = carve(2 * 2 * D)
        er_e = carve(4 * D)
        er_r = carve(4 * D)
        stage_w = sb("stage_w", [P, 2048])
        b2_rows = carve(E * D, 0)
        b2_hi = carve(E * D // 2).bitcast(F16)
        comb = carve(8 * D, 5120)
        junk = carve(2 * D)
        y32 = carve(4 * D, 0)
        y16 = carve(8 * D).bitcast(F16)
        yT = carve(2 * 2 * D)
        lg, eqm, sc, M1, M2, lg2, pf, big_a, big_b, onesd = (carve(512, 0 if k == 0 else None) for k in range(10))
        cmp_t = carve(SLOTS * E)
        msum = carve(256).bitcast(F16)
        inv_a = carve(4 * P)
        inv_b = carve(4 * SLOTS)
        gat = carve(4 * D, 0).bitcast(F16)
        tT = carve(4 * D).bitcast(F16)
        hid = carve(2 * 512)
        hid_hi = carve(512).bitcast(F16)
        hid_lo = carve(512).bitcast(F16)
        o_sb = carve(4 * D)

        bank = [ctx.enter_context(nc.psum_tensor(f"bank{k}", [P, 512], F32)) for k in range(8)]

        go = sem("go")
        pool_tick = sem("pool_tick")
        const_pool = sem("const_pool")
        const_ready = sem("const_ready")
        small_in = sem("small_in")
        b2_in = sem("b2_in")
        setup_dve = sem("setup_dve")
        setup_mm = sem("setup_mm")
        x_loaded = [sem(f"x_loaded_{k}") for k in range(4)]
        adj_loaded, weights_loaded, out_stored = sem2("adj_loaded"), sem2("weights_loaded"), sem("out_stored")
        y_stored = [sem2(f"y_stored_{k}") for k in range(2)]
        gathered = [sem(f"gathered_{k}") for k in range(SU)]
        stored = [sem(f"stored_{k}") for k in range(SU)]
        c_gathered = [sem(f"c_gathered_{k}") for k in range(8)]
        own = sem("dve_own")
        neg_ready, diag_ready, scaled, split_done, x_plus_y, idx_ready, cidx_ready = by_pool = [sem2(n) for n in (
            "neg_ready", "diag_ready", "scaled", "split_done", "x_plus_y", "idx_ready", "cidx_ready")]
        E_mm, PT_mm, G_mm, H_mm, yT_mm, logit_mm, rank_mm, inv_mm, T_mm, h_mm, o_mm = by_pe = [sem2(n) for n in (
            "E_mm", "PT_mm", "G_mm", "H_mm", "yT_mm", "logit_mm", "rank_mm", "inv_mm", "T_mm", "h_mm", "o_mm")]
        E_ev, exp_done, PT_ev, G_ev, e_done, ER_done, yT_ev, sd_ready, e2_ready, h_act, o_ev = by_act = [sem2(n) for n in (
            "E_ev", "exp_done", "PT_ev", "G_ev", "e_done", "ER_done", "yT_ev", "sd_ready", "e2_ready", "h_act", "o_ev")]
        (combined, var_ready, s_ready, sm_ready, xn_ready, post, rinv_ready, y_ready, hi_ready, yl_ready, gap_ready,
         msum_ready, ab_ready, slots_ready, T_ev, h_split) = by_dve = [sem2(n) for n in (
            "combined", "var_ready", "s_ready", "sm_ready", "xn_ready", "post", "rinv_ready", "y_ready", "hi_ready",
            "yl_ready", "gap_ready", "msum_ready", "ab_ready", "slots_ready", "T_ev", "h_split")]

        def credit(eng, sems):
            for pair in sems:
                for s in pair:
                    eng.sem_inc(s, AHEAD)

        def loop_wait(eng, s, value):
            eng.wait_ge(s, value)
            eng.wait_ge(go, 1)

        class Chain:

            def __init__(self, eng, s):
                self.eng, self.s, self.n, self.base = eng, s, 0, 0

            def mark(self, ins):
                ins.then_inc(self.s, 1)
                self.n += 1
                return self.n

            def wait(self, n=None):
                loop_wait(self.eng, self.s, self.base + (self.n if n is None else n))

            def enter(self, i, per_turn):
                self.base, self.start, self.per = i * per_turn, self.n, per_turn

            def leave(self, turns):
                assert self.n - self.start == self.per, (self.n - self.start, self.per)
                self.base, self.n = 0, self.start + self.per * turns

        block = ctx.enter_context(nc.Block())

        xt_dram = x_in.rearrange("(t two) n d -> (two n) t d", two=2)
        out_dram = out.rearrange("(t two) n d -> (two n) t d", two=2)
        adj_dram = adj.rearrange("(t two) i j -> (two i) t j", two=2)
        TURNS = SLOTS // SU

        def cut(a, start, n):
            return a[:, start:start + n] if isinstance(start, int) else a[:, bass.ds(start, n)]

        def xs(t, n=1):
            return cut(X, t * D, n * D)

        def one(name, t, n=1):
            return cut(cols, names.index(name) * TILES + t, n)

        def bc(a, n):
            return a.rearrange("p (m one) -> p m one", one=1).to_broadcast([P, a.shape[1], n])

        def rows(a, n):
            return a.rearrange("p (one m) -> p one m", one=1).to_broadcast([P, n, a.shape[1]])

        def w1_at(L, e, hl, kc, fc):
            return cut(WREG, e * (8 * HID[L]) + ((hl * KC + kc) * HID[L] + fc * P), P)

        def w2_at(L, e, hl, fc):
            return cut(WREG, e * (8 * HID[L]) + (4 * HID[L] + (hl * (HID[L] // P) + fc) * D), D)

        def combine_gathers(pool, L):
            for u in range(SU):
                pool.wait_ge(stored[u], 16 + 16 * TURNS * (L + 1))
            with pool.Fori(0, TILES // 4) as i:
                for u in range(4):
                    for k in range(TOPK):
                        b = 2 * u + k
                        loop_wait(pool, combined[L], at(i * 4 + u - 4 + 1))
                        nc.gpsimd.tensor_copy(index_now[:, b:b + 1], cut(pos_i[k], i * 4 + u, 1).bitcast(U32)).then_inc(cidx_ready[L], 1)
                        pool.wait_ge(cidx_ready[L], at(i * 8 + b + 1))
                        pool.sem_inc(pool_tick)
                        nc.gpsimd.indirect_dma_start(
                            out=comb[:, b * D:(b + 1) * D], out_offset=None, in_=ydram[L],
                            in_offset=bass.IndirectOffsetOnAxis(ap=index_now[:, b:b + 1], axis=0)).then_inc(c_gathered[b], 16)

        def combine(dve, ch, L, stats_too):
            V = nc.vector
            with dve.Fori(0, TILES // 4) as i:
                ch.enter(i, 4 * (1 + (3 if stats_too else 0)))
                for u in range(4):
                    t = i * 4 + u
                    for k in range(TOPK):
                        loop_wait(dve, c_gathered[2 * u + k], 16 * (TILES // 4) * L + i * 16 + 16)
                        ins = V.scalar_tensor_tensor(xs(t), comb[:, (2 * u + k) * D:(2 * u + k + 1) * D],
                                                     one(f"w{k + 1}", t), xs(t), ALU.mult, ALU.add)
                        if k == 0:
                            ch.mark(ins)
                            ch.wait()
                        else:
                            ins.then_inc(combined[L], 1)
                    if stats_too:
                        loop_wait(dve, combined[L], at(t + 1))
                        ch.mark(V.bn_stats(cut(stats, t * 6, 6), xs(t)))
                        for j in range(2):
                            ch.mark(V.scalar_tensor_tensor(junk[:, j * D:(j + 1) * D], xs(t), 1.0, u_bc[:, j * D:(j + 1) * D],
                                                           ALU.mult, ALU.mult, accum_out=one(f"dot{j + 1}", t)))
            ch.leave(TILES // 4)

        @block.sync
        def _(sp):
            sp.sem_inc(go, 1)
            for u in range(SU):
                sp.sem_inc(stored[u], 16)
            for L in range(2):
                sp.dma_start(wg_sb[:, L * KC * D:(L + 1) * KC * D].rearrange("p (k n) -> p k n", k=KC),
                             W_gnn[L].rearrange("(k p) n -> p k n", p=P)).then_inc(small_in, 16)
                with nc.allow_non_contiguous_dma(reason="vectors onto partitions"):
                    sp.dma_start(a_cols[:, L * 4:(L + 1) * 4],
                                 a_gnn[L].rearrange("(k p) one -> p (k one)", p=P)).then_inc(small_in, 16)
                    base = L * E * HID[0] // P
                    sp.dma_start(b1T[:, base:base + E * HID[L] // P].rearrange("p (e c) -> p e c", e=E),
                                 b1[L].rearrange("e (c p) -> p e c", p=P)).then_inc(small_in, 16)
            sp.dma_start(rt_rows[:], router[0]).then_inc(small_in, 16)
            sp.dma_start(rt_sb[:, KC * E:2 * KC * E].rearrange("p (k n) -> p k n", k=KC),
                         router[1].rearrange("(k p) n -> p k n", p=P)).then_inc(small_in, 16)
            for k, v in enumerate((gate_b, gate_bias)):
                sp.dma_start(gb_bc[:, k * E:(k + 1) * E],
                             v.rearrange("(one e) -> one e", one=1).to_broadcast([P, E])).then_inc(small_in, 16)
            sp.wait_ge(const_ready, 1)
            for k in range(4):
                sp.dma_start(b2_rows[32 * k:32 * k + 1, :],
                             b2[k // 2].rearrange("(one e) d -> one (e d)", one=1)).then_inc(b2_in, 16)
            for c in range(TILES // 4):
                if c >= 4:
                    sp.wait_ge(x_loaded[c % 4], 16 * (c // 4))
                sp.dma_start(xs(4 * c, 4).rearrange("p (t d) -> p t d", d=D),
                             xt_dram[:, 4 * c:4 * c + 4, :]).then_inc(x_loaded[c % 4], 16)

            for L in range(2):
                F = HID[L]
                if L == 0:
                    sp.wait_ge(s_ready[0], at(1))
                else:
                    sp.wait_ge(combined[0], at(TILES))
                with sp.Fori(0, GROUPS) as g:
                    sp.wait_ge(neg_ready[L], at(g))
                    sp.dma_start(adj_sb.rearrange("p (t j) -> p t j", t=GT),
                                 adj_dram[:, bass.ds(g * GT, GT), :]).then_inc(adj_loaded[L], 16)
                    sp.wait_ge(split_done[L], at(g))
                    sp.dma_start(stage_w[:, 0:KC * F].rearrange("p (k f) -> p k f", k=KC),
                                 w1[L].rearrange("e (k p) f -> p (e k) f", p=P)[:, bass.ds(g * KC, KC), :]).then_inc(weights_loaded[L], 16)
                    sp.dma_start(stage_w[:, KC * F:4 * F].rearrange("p (k n) -> p k n", k=F // P),
                                 w2[L].rearrange("e (k p) n -> p (e k) n", p=P)[:, bass.ds(g * (F // P), F // P), :]).then_inc(weights_loaded[L], 16)
                with sp.Fori(0, TILES // 8) as i:
                    for h in range(2):
                        sp.wait_ge(yl_ready[L], at(i * 8 + 4 * h + 4))
                        sp.dma_start(table[L].rearrange("(t p) c -> p t c", p=P)[:, bass.ds(i * 8 + 4 * h, 4), :],
                                     y16[:, 4 * h * 512:(4 * h + 4) * 512].rearrange("p (t c) -> p t c", t=4)).then_inc(y_stored[h][L], 16)
                with sp.Fori(0, TURNS) as i:
                    for u in range(SU):
                        sp.wait_ge(o_ev[L], at(i * SU + u + 1))
                        sp.dma_start(ydram[L][bass.ds((i * SU + u) * P, P), :],
                                     o_sb[:, u * D:(u + 1) * D]).then_inc(stored[u], 16)
            with sp.Fori(0, TILES // 4) as i:
                sp.wait_ge(combined[1], at(i * 4 + 4))
                sp.dma_start(out_dram[:, bass.ds(i * 4, 4), :], xs(i * 4, 4).rearrange("p (t d) -> p t d", d=D)).then_inc(out_stored, 16)
            sp.wait_ge(out_stored, 16 * (TILES // 4))

        @block.gpsimd
        def _(pool):
            credit(pool, by_pool)
            n = 0

            def step(ins):
                nonlocal n
                n += 1
                ins.then_inc(const_pool, 1)
                pool.wait_ge(const_pool, n)

            for t_, v in ((ident, 0.0), (ident16, 0.0), (before16, 1.0), (same_graph, 0.0), (stacked_id, 0.0),
                          (ones16, 1.0), (eps_col, EPS), (b2_pick, 0.0), (b2_low64, 0.0), (b2_sign, 1.0)):
                step(nc.gpsimd.memset(t_[:], v))
            step(nc.gpsimd.memset(b2_rows, 0.0))
            for t_ in (ident, ident16):
                step(nc.gpsimd.affine_select(out=t_[:], in_=t_[:], compare_op=ALU.not_equal, fill=1.0, base=0,
                                             pattern=[[-1, P]], channel_multiplier=1))
            step(nc.gpsimd.affine_select(out=before16[:], in_=before16[:], compare_op=ALU.is_gt, fill=0.0, base=0,
                                         pattern=[[1, P]], channel_multiplier=-1))
            step(nc.gpsimd.memset(same_graph[0:NODES, 0:NODES], 1.0))
            step(nc.gpsimd.memset(same_graph[NODES:P, NODES:P], 1.0))
            for k in range(4):
                step(nc.gpsimd.memset(b2_pick[32 * k:32 * k + 1, (k // 2) * P:(k // 2 + 1) * P], 1.0))
                if k % 2:
                    step(nc.gpsimd.memset(b2_low64[32 * k:32 * k + 1, :], WSCALE))
                    step(nc.gpsimd.memset(b2_sign[32 * k:32 * k + 1, :], -1.0))
            for b in (0, NODES):
                step(nc.gpsimd.affine_select(out=stacked_id[:], in_=stacked_id[:], compare_op=ALU.not_equal, fill=1.0,
                                             base=-b, pattern=[[-1, NODES]], channel_multiplier=1))
            for t_, pat, base, cm in ((iota_p, [[1, P]], 0, 0), (iota_s, [[1, SLOTS]], 0, 0),
                                      (token_id, [[P, TILES]], 0, 1), (rank8, [[-1, E]], E, 0)):
                step(nc.gpsimd.iota(t_[:], pattern=pat, base=base, channel_multiplier=cm,
                                    allow_small_or_imprecise_dtypes=True))
            nc.gpsimd.memset(index_now[:], 0).then_inc(const_ready, 1)

            for L in range(2):
                F = HID[L]
                if L == 1:
                    combine_gathers(pool, 0)
                with pool.Fori(0, GROUPS) as g:
                    pool.wait_ge(sm_ready[L], at(g))
                    pool.wait_ge(adj_loaded[L], g * 16 + 16)
                    pool.sem_inc(pool_tick)
                    nc.gpsimd.tensor_scalar(neg, adj_sb, 0, NEG_BIG, ALU.is_le, ALU.mult).then_inc(neg_ready[L], 1)
                    pool.wait_ge(s_ready[L], at(1))
                    loop_wait(pool, E_mm[L], at(g))
                    nc.gpsimd.tensor_tensor(diag.rearrange("p (t j) -> p t j", t=GT), rows(stacked_id[:], GT),
                                            bc(one("s2", g * GT, GT), NODES), ALU.mult).then_inc(diag_ready[L], 1)
                    pool.wait_ge(weights_loaded[L], g * 32 + 32)
                    pool.sem_inc(pool_tick)
                    nc.gpsimd.tensor_scalar(stage_w[:, 0:4 * F], stage_w[:, 0:4 * F], WSCALE, None, ALU.mult).then_inc(scaled[L], 1)
                    parts = ((0, 2 * F, 0), (2 * F, 2 * F, 4 * F))
                    loop_wait(pool, scaled[L], at(g * 3 + 1))
                    for src, ln, dst in parts:
                        nc.gpsimd.tensor_copy(cut(WREG, g * (8 * F) + dst, ln), stage_w[:, src:src + ln]).then_inc(scaled[L], 1)
                    loop_wait(pool, scaled[L], at(g * 3 + 3))
                    for src, ln, dst in parts:
                        ins = nc.gpsimd.tensor_tensor(cut(WREG, g * (8 * F) + dst + ln, ln), stage_w[:, src:src + ln],
                                                      cut(WREG, g * (8 * F) + dst, ln), ALU.subtract)
                    ins.then_inc(split_done[L], 1)
                if L == 0:
                    with pool.Fori(0, TILES // 4) as i:
                        for u in range(4):
                            loop_wait(pool, y_ready[L], at(i * 4 + u + 1))
                            nc.gpsimd.tensor_tensor(xs(i * 4 + u), xs(i * 4 + u), y32[:, u * D:(u + 1) * D],
                                                    ALU.add).then_inc(x_plus_y[L], 1)
                for h in range(2):
                    pool.wait_ge(y_stored[h][L], 16 * (TILES // 8))
                pool.wait_ge(slots_ready[L], at(1))
                with pool.Fori(0, TURNS) as i:
                    for u in range(SU):
                        s = i * SU + u
                        loop_wait(pool, T_mm[L], at(s - SU + 1))
                        nc.gpsimd.tensor_copy(index_now[:, u:u + 1], slot_token[:, bass.ds(s, 1)]).then_inc(idx_ready[L], 1)
                        pool.wait_ge(idx_ready[L], at(s + 1))
                        pool.sem_inc(pool_tick)
                        nc.gpsimd.indirect_dma_start(
                            out=gat[:, u * 512:(u + 1) * 512], out_offset=None, in_=table[L],
                            in_offset=bass.IndirectOffsetOnAxis(ap=index_now[:, u:u + 1], axis=0)).then_inc(gathered[u], 16)
            combine_gathers(pool, 1)

        @block.tensor
        def _(pe):
            credit(pe, by_pe)
            mm = nc.tensor.matmul
            pe.wait_ge(const_ready, 1)
            pe.wait_ge(small_in, 16 * 10)
            for c in range(KC):
                last = nc.tensor.transpose(bank[2][:, c * E:(c + 1) * E], rt_rows[:, c * P:(c + 1) * P], ident[0:E, 0:E])
            last.then_inc(setup_mm, 1)

            def edge_vectors(L):
                for oc in range(KC):
                    for fc in range(KC):
                        last = nc.tensor.transpose(bank[0][:, oc * D + fc * P:oc * D + (fc + 1) * P],
                                                   wg_sb[:, (L * KC + fc) * D + oc * P:(L * KC + fc) * D + (oc + 1) * P], ident[:])
                last.then_inc(setup_mm, 1)
                pe.wait_ge(setup_dve, 2 + 2 * L + 1)
                for j in range(2):
                    for oc in range(KC):
                        last = mm(bank[1][:, j * D:(j + 1) * D], abc[:, (2 * j + oc) * P:(2 * j + oc + 1) * P],
                                  wgT[:, oc * D:(oc + 1) * D], start=oc == 0, stop=oc == KC - 1)
                last.then_inc(setup_mm, 1)

            def scores_of(L, g):
                loop_wait(pe, diag_ready[L], at(g + 1))
                loop_wait(pe, E_ev[L], at(g))
                mm(bank[0][:], same_graph[:], diag[:], start=True, stop=False)
                mm(bank[0][:].rearrange("p (t j) -> p t j", t=GT), ident[:], bc(one("s1", g * GT, GT), NODES),
                   start=False, stop=True).then_inc(E_mm[L], 1)

            def attend(L, g, more):
                if more:
                    scores_of(L, g + 1)
                for h in range(2):
                    if h == 0:
                        loop_wait(pe, exp_done[L], at(g + 1))
                    loop_wait(pe, PT_ev[L], at(2 * g + h - 1))
                    for j in range(4):
                        last = nc.tensor.transpose(bank[1 + h][:, j * P:(j + 1) * P],
                                                   probs[:, (4 * h + j) * P:(4 * h + j + 1) * P], ident[:])
                    last.then_inc(PT_mm[L], 1)

                def aggregate(q):
                    if q == 0:
                        loop_wait(pe, xn_ready[L], at(g + 1))
                    if q % 2 == 0:
                        loop_wait(pe, PT_ev[L], at(2 * g + q // 2 + 1))
                    loop_wait(pe, G_ev[L], at(4 * g + q - 1))
                    for a in range(2):
                        for c in range(KC):
                            j = 2 * q + a
                            last = mm(bank[3 + q % 2][:, (2 * a + c) * P:(2 * a + c + 1) * P],
                                      xn[:, j * D + c * P:j * D + (c + 1) * P], probsT[:, j * P:(j + 1) * P],
                                      start=True, stop=True)
                    last.then_inc(G_mm[L], 1)

                def project(q):
                    loop_wait(pe, G_ev[L], at(4 * g + q + 1))
                    loop_wait(pe, ER_done[L], at(8 * g + 2 * q - 2))
                    for a in range(2):
                        for c in range(KC):
                            o = (q % 2) * 2 * D + a * D + c * P
                            last = mm(bank[5 + q % 2][:, a * D:(a + 1) * D], gT[:, o:o + P],
                                      wg_sb[:, (L * KC + c) * D:(L * KC + c + 1) * D], start=c == 0, stop=c == KC - 1)
                    last.then_inc(H_mm[L], 1)

                aggregate(0)
                aggregate(1)
                project(0)
                aggregate(2)
                project(1)
                aggregate(3)
                project(2)
                project(3)

            for L in range(2):
                F = HID[L]
                FC = F // P
                edge_vectors(L)
                scores_of(L, 0)
                with pe.Fori(0, GROUPS - 1) as g:
                    attend(L, g, True)
                attend(L, GROUPS - 1, False)

                with pe.Fori(0, TILES // 4) as i:
                    for q in range(2):
                        loop_wait(pe, y_ready[L], at(4 * i + 2 * q + 2))
                        loop_wait(pe, yT_ev[L], at(2 * i + q - 1))
                        for a in range(2):
                            for c in range(KC):
                                last = nc.tensor.transpose(bank[q][:, (2 * a + c) * P:(2 * a + c + 1) * P],
                                                           y32[:, (2 * q + a) * D + c * P:(2 * q + a) * D + (c + 1) * P], ident[:])
                        last.then_inc(yT_mm[L], 1)
                    for q in range(2):
                        loop_wait(pe, yT_ev[L], at(2 * i + q + 1))
                        for a in range(2):
                            for c in range(KC):
                                last = mm(bank[7][:, bass.ds((4 * i + 2 * q + a) * E, E)],
                                          yT[:, q * 2 * D + (2 * a + c) * P:q * 2 * D + (2 * a + c + 1) * P],
                                          rt_sb[:, (L * KC + c) * E:(L * KC + c + 1) * E], start=c == 0, stop=c == KC - 1)
                        last.then_inc(logit_mm[L], 1)

                pe.wait_ge(msum_ready[L], at(1))
                mm(bank[0][:], before16[:], msum[:, 0:512], start=True, stop=True)
                mm(bank[1][:], ones16[:], msum[:, 0:512], start=True, stop=True).then_inc(rank_mm[L], 1)
                pe.wait_ge(ab_ready[L], at(1))
                mm(bank[2][:, 0:SLOTS], inv_a[:, 0:P], inv_b[:, 0:SLOTS], start=True, stop=False).then_inc(inv_mm[L], 1)
                with pe.Fori(0, TILES // 2) as i:
                    for b in range(4):
                        pe.wait_ge(ab_ready[L], at(4 * i + b + 2))
                        last = mm(bank[2][:, 0:SLOTS], inv_a[:, b * P:(b + 1) * P], inv_b[:, b * SLOTS:(b + 1) * SLOTS],
                                  start=False, stop=False)
                        last.then_inc(inv_mm[L], 1)
                pe.wait_ge(ab_ready[L], at(2 * TILES + 2))
                mm(bank[2][:, 0:SLOTS], inv_a[:, 0:P], inv_b[:, 0:SLOTS], start=False, stop=True).then_inc(inv_mm[L], 1)

                def turn_over(s, u):
                    pe.wait_ge(gathered[u % SU], 16 * TURNS * L + 16 * (s[1] + 1))
                    loop_wait(pe, T_ev[L], at(s[0] - 1))
                    for j in range(4):
                        last = nc.tensor.transpose(bank[u % 2][:, j * (P // 2):(j + 1) * (P // 2)].bitcast(F16),
                                                   gat[:, (u % SU) * 512 + j * P:(u % SU) * 512 + (j + 1) * P], ident16[:])
                    last.then_inc(T_mm[L], 1)

                def hidden(s, u, e):
                    loop_wait(pe, T_ev[L], at(s + 1))
                    loop_wait(pe, h_act[L], at(s - 1))
                    tb = (u % SU) * 512
                    for fc in range(FC):
                        n = 0
                        for kc in range(KC):
                            for wh, yh in ((0, 0), (0, 1), (1, 0)):
                                last = mm(bank[2 + u % 2][:, fc * P:(fc + 1) * P], w1_at(L, e, wh, kc, fc),
                                          tT[:, tb + (yh * KC + kc) * P:tb + (yh * KC + kc + 1) * P],
                                          start=n == 0, stop=n == 3 * KC - 1)
                                n += 1
                    last.then_inc(h_mm[L], 1)

                def output(s, u, e):
                    loop_wait(pe, h_split[L], at(s + 1))
                    loop_wait(pe, o_ev[L], at(s - 1))
                    hb = (u % 2) * 512
                    ob = bank[4 + u % 2][:, 0:D]
                    mm(ob, b2_pick[:, L * P:(L + 1) * P], cut(b2_pair, e * D, D), start=True, stop=False)
                    for fc in range(FC):
                        for hsrc, wh in ((hid_hi, 0), (hid_hi, 1), (hid_lo, 0)):
                            last = mm(ob, hsrc[:, hb + fc * P:hb + (fc + 1) * P], w2_at(L, e, wh, fc),
                                      start=False, stop=fc == FC - 1 and hsrc is hid_lo)
                    last.then_inc(o_mm[L], 1)

                def experts(i, more):
                    es = [pe.value_load(slot_expert[0:1, i * SU + u:i * SU + u + 1] if isinstance(i, int) else
                                        slot_expert[0:1, bass.ds(i * SU + u, 1)], min_val=0, max_val=E - 1)
                          for u in range(SU + (1 if more else 0))]
                    for u in range(SU):
                        s = i * SU + u
                        if more or u + 2 < SU:
                            turn_over((s + 2, i + (u + 2) // SU), u + 2)
                        if more or u + 1 < SU:
                            hidden(s + 1, u + 1, es[u + 1])
                        output(s, u, es[u])

                pe.wait_ge(slots_ready[L], at(1))
                turn_over((0, 0), 0)
                turn_over((1, 0), 1)
                hidden(0, 0, pe.value_load(slot_expert[0:1, 0:1], min_val=0, max_val=E - 1))
                with pe.Fori(0, TURNS - 1) as i:
                    experts(i, True)
                experts(TURNS - 1, False)

        @block.scalar
        def _(act):
            credit(act, by_act)
            A = nc.scalar.activation

            def copy_scores(L, g):
                loop_wait(act, E_mm[L], at(g + 1))
                loop_wait(act, exp_done[L], at(g))
                A(scores, bank[0][:], ACT.Copy).then_inc(E_ev[L], 1)

            def exponent(L, g):
                loop_wait(act, sm_ready[L], at(g + 1))
                loop_wait(act, PT_mm[L], at(2 * g))
                loop_wait(act, rinv_ready[L], at(g))
                for r in range(2):
                    pr = slice(r * NODES, (r + 1) * NODES)
                    ins = A(probs.rearrange("p (t c) -> p t c", t=GT)[pr, :, r * NODES:(r + 1) * NODES],
                            scores.rearrange("p (t j) -> p t j", t=GT)[pr, :, :], ACT.Exp)
                ins.then_inc(exp_done[L], 1)

            def attend(L, g, more):
                if more:
                    copy_scores(L, g + 1)
                for h in range(2):
                    loop_wait(act, PT_mm[L], at(2 * g + h + 1))
                    loop_wait(act, G_mm[L], at(4 * g))
                    A(probsT[:, h * 512:(h + 1) * 512], bank[1 + h][:], ACT.Copy).then_inc(PT_ev[L], 1)

                def copy_g(q):
                    loop_wait(act, G_mm[L], at(4 * g + q + 1))
                    loop_wait(act, H_mm[L], at(4 * g + q - 1))
                    A(gT[:, (q % 2) * 512:(q % 2 + 1) * 512], bank[3 + q % 2][:], ACT.Copy).then_inc(G_ev[L], 1)

                def elu_parts(q):
                    for a in range(2):
                        j = 2 * q + a
                        if a == 0:
                            loop_wait(act, H_mm[L], at(4 * g + q + 1))
                            if q == 0:
                                loop_wait(act, rinv_ready[L], at(g + 1))
                        loop_wait(act, post[L], at(8 * g + j - 3))
                        src = bank[5 + q % 2][:, a * D:(a + 1) * D]
                        b = (j % 4) * D
                        A(er_e[:, b:b + D], src, ACT.Exp, scale=rinv[:, j:j + 1]).then_inc(e_done[L], 1)
                        A(er_r[:, b:b + D], src, ACT.Relu, scale=rinv[:, j:j + 1]).then_inc(ER_done[L], 1)

                copy_g(0)
                copy_g(1)
                elu_parts(0)
                copy_g(2)
                elu_parts(1)
                if more:
                    exponent(L, g + 1)
                copy_g(3)
                elu_parts(2)
                elu_parts(3)

            for L in range(2):
                F = HID[L]
                FC = F // P
                act.wait_ge(var_ready[L], at(1))
                A(col["sd"], col["var"], ACT.Sqrt, bias=eps_col[:]).then_inc(sd_ready[L], 1)
                copy_scores(L, 0)
                exponent(L, 0)
                with act.Fori(0, GROUPS - 1) as g:
                    attend(L, g, True)
                attend(L, GROUPS - 1, False)
                act.wait_ge(var_ready[L], at(2))
                A(col["sd"], col["var"], ACT.Sqrt, bias=eps_col[:]).then_inc(sd_ready[L], 1)
                with act.Fori(0, TILES // 4) as i:
                    for q in range(2):
                        loop_wait(act, yT_mm[L], at(2 * i + q + 1))
                        loop_wait(act, logit_mm[L], at(2 * i + q - 1))
                        A(yT[:, q * 512:(q + 1) * 512], bank[q][:], ACT.Copy).then_inc(yT_ev[L], 1)
                act.wait_ge(gap_ready[L], at(1))
                A(col["ta"], col["tb"], ACT.Exp).then_inc(e2_ready[L], 1)

                def activate(s, u, e):
                    loop_wait(act, h_mm[L], at(s + 1))
                    loop_wait(act, h_split[L], at(s - 1))
                    base = L * E * HID[0] // P
                    for fc in range(FC):
                        ins = A(hid[:, (u % 2) * 512 + fc * P:(u % 2) * 512 + (fc + 1) * P], bank[2 + u % 2][:, fc * P:(fc + 1) * P],
                                ACT.Gelu if L == 0 else ACT.Relu, bias=cut(b1T, e * FC + (base + fc), 1), scale=1.0 / WSCALE)
                    ins.then_inc(h_act[L], 1)

                def copy_out(s, u, i):
                    loop_wait(act, o_mm[L], at(s + 1))
                    loop_wait(act, stored[u], 16 + 16 * TURNS * L + 16 * i)
                    A(o_sb[:, u * D:(u + 1) * D], bank[4 + u % 2][:, 0:D], ACT.Copy, scale=1.0 / WSCALE).then_inc(o_ev[L], 1)

                def experts(i, more):
                    es = [None] + [act.value_load(cut(slot_expert, i * SU + u, 1), min_val=0, max_val=E - 1)
                                   for u in range(1, SU + (1 if more else 0))]
                    for u in range(SU):
                        s = i * SU + u
                        if more or u + 1 < SU:
                            activate(s + 1, u + 1, es[u + 1])
                        copy_out(s, u, i)

                act.wait_ge(slots_ready[L], at(1))
                activate(0, 0, act.value_load(slot_expert[0:1, 0:1], min_val=0, max_val=E - 1))
                with act.Fori(0, TURNS - 1) as i:
                    experts(i, True)
                experts(TURNS - 1, False)

        @block.vector
        def _(dve):
            credit(dve, by_dve)
            V = nc.vector
            ch = Chain(dve, own)
            tt, stt, ts = V.tensor_tensor, V.scalar_tensor_tensor, V.tensor_scalar
            stats3 = stats[:].rearrange("p (t s) -> p t s", s=6)

            def st(k):
                return stats3[:, :, k:k + 1].rearrange("p t one -> p (t one)")

            dve.wait_ge(const_ready, 1)
            dve.wait_ge(b2_in, 64)
            ch.mark(ts(b2_hi, b2_rows, WSCALE, None, ALU.mult))
            ch.wait()
            ch.mark(ts(b2_rows, b2_rows, b2_low64[:], None, ALU.mult))
            ch.wait()
            stt(b2_pair[:], b2_hi, b2_sign[:], b2_rows, ALU.mult, ALU.add).then_inc(setup_dve, 1)
            dve.wait_ge(small_in, 16 * 10)
            dve.wait_ge(setup_mm, 1)
            V.tensor_copy(rt_sb[:, 0:KC * E], bank[2][:, 0:KC * E]).then_inc(setup_dve, 1)

            def token_stats(L, t, k):
                V.bn_stats(cut(stats, t * 6, 6), xs(t))

            def dots(t, jb):
                for j in range(2):
                    ch.mark(stt(junk[:, j * D:(j + 1) * D], xs(t), 1.0, u_bc[:, j * D:(j + 1) * D], ALU.mult, ALU.mult,
                                accum_out=one(f"dot{j + 1}", t)))

            def mean_var(L):
                ch.mark(tt(col["ta"], st(1), st(4), ALU.add))
                ch.mark(tt(col["tb"], st(1), st(4), ALU.subtract))
                ch.mark(tt(col["tc"], st(2), st(5), ALU.add))
                ch.wait()
                ch.mark(ts(col["mean"], col["ta"], 0.5, None, ALU.mult))
                ch.mark(stt(col["td"], col["tb"], 0.25, col["tb"], ALU.mult, ALU.mult))
                ch.wait()
                stt(col["var"], col["tc"], 1.0 / D, col["td"], ALU.mult, ALU.add).then_inc(var_ready[L], 1)

            def rstd_of(L, n, r, m):
                dve.wait_ge(sd_ready[L], at(n))
                ch.mark(V.reciprocal(col[r], col["sd"]))
                ch.wait()
                ch.mark(stt(col[m], col["mean"], -1.0, col[r], ALU.mult, ALU.mult))
                ch.wait()

            def soft(L, g):
                loop_wait(dve, E_ev[L], at(g + 1))
                loop_wait(dve, neg_ready[L], at(g + 1))
                if L == 1:
                    ch.mark(stt(scores, scores, LEAK, scores, ALU.mult, ALU.max))
                    ch.wait()
                ch.mark(tt(scores, scores, neg, ALU.add))
                ch.wait()
                s3 = scores.rearrange("p (t j) -> p t j", t=GT)
                ch.mark(V.tensor_reduce(rinv[:, GT:2 * GT], s3, AX.X, ALU.max))
                ch.wait()
                tt(s3, s3, bc(rinv[:, GT:2 * GT], NODES), ALU.subtract).then_inc(sm_ready[L], 1)

            def tokens_of(L, g):
                loop_wait(dve, G_mm[L], at(4 * g))
                for j in range(GT):
                    ins = ts(xn[:, j * D:(j + 1) * D], xs(g * GT + j), one("rstd", g * GT + j), one("nmr", g * GT + j), ALU.mult, ALU.add)
                    if j == GT - 1:
                        ins.then_inc(xn_ready[L], 1)
                loop_wait(dve, exp_done[L], at(g + 1))
                ch.mark(V.tensor_reduce(rinv[:, GT:2 * GT], probs.rearrange("p (t j) -> p t j", t=GT), AX.X, ALU.add))
                ch.wait()
                V.reciprocal(rinv[:, 0:GT], rinv[:, GT:2 * GT]).then_inc(rinv_ready[L], 1)

            def attend(L, g, more):
                if more:
                    soft(L, g + 1)
                for j in range(GT + 1):
                    if j < GT:
                        b = (j % 4) * D
                        loop_wait(dve, ER_done[L], at(8 * g + j + 1))
                        ch.mark(stt(er_e[:, b:b + D], er_e[:, b:b + D], 1.0, er_r[:, b:b + D], ALU.min, ALU.add))
                        ch.wait()
                        t = g * GT + j
                        stt(xs(t), er_e[:, b:b + D], -1.0, xs(t), ALU.add, ALU.add).then_inc(post[L], 1)
                        loop_wait(dve, post[L], at(8 * g + j + 1))
                        ch.mark(V.bn_stats(cut(stats, t * 6, 6), xs(t)))
                if more:
                    tokens_of(L, g + 1)

            PER_ATTEND = 2 + 2 * GT + 1
            for L in range(2):
                F = HID[L]
                FC = F // P
                for k in range(4):
                    ch.mark(V.tensor_copy(abc[:, k * P:(k + 1) * P], a_cols[:, L * 4 + k:L * 4 + k + 1].to_broadcast([P, P])))
                dve.wait_ge(setup_mm, 2 + 2 * L)
                V.tensor_copy(wgT[:], bank[0][:]).then_inc(setup_dve, 1)
                dve.wait_ge(setup_mm, 3 + 2 * L)
                ch.wait()
                V.tensor_copy(u_bc[:], bank[1][:]).then_inc(setup_dve, 1)
                dve.wait_ge(setup_dve, 4 + 2 * L)
                ch.mark(V.tensor_reduce(u_sum[:], u_bc[:].rearrange("p (j d) -> p j d", j=2), AX.X, ALU.add))

                if L == 0:
                    with dve.Fori(0, TILES // 16) as i:
                        ch.enter(i, 3 * 16)
                        for c in range(4):
                            loop_wait(dve, x_loaded[c], i * 16 + 16)
                            for v in range(4):
                                t = i * 16 + 4 * c + v
                                ch.mark(V.bn_stats(cut(stats, t * 6, 6), xs(t)))
                                ch.wait()
                                dots(t, v)
                    ch.leave(TILES // 16)
                else:
                    combine(dve, ch, 0, True)
                ch.wait()
                ch.mark(V.memset(probs, 0.0))
                mean_var(L)
                rstd_of(L, 1, "rstd", "nmr")
                for j in range(2):
                    ch.mark(tt(col["ta"], col[f"dot{j + 1}"], col["rstd"], ALU.mult))
                    ch.wait()
                    ins = stt(col[f"s{j + 1}"], col["nmr"], u_sum[:, j:j + 1], col["ta"], ALU.mult, ALU.add)
                    if j == 0:
                        ch.mark(ins)
                        ch.wait()
                    else:
                        ins.then_inc(s_ready[L], 1)

                soft(L, 0)
                tokens_of(L, 0)
                with dve.Fori(0, GROUPS - 1) as g:
                    ch.enter(g, PER_ATTEND + L)
                    attend(L, g, True)
                ch.leave(GROUPS - 1)
                attend(L, GROUPS - 1, False)

                ch.wait()
                mean_var(L)
                rstd_of(L, 2, "rs2", "nm2")
                with dve.Fori(0, TILES // 8) as i:
                    for v in range(8):
                        t = i * 8 + v
                        b = (v % 4) * D
                        loop_wait(dve, yT_mm[L], at(i * 4 + v // 2 - 1))
                        if L == 0:
                            loop_wait(dve, x_plus_y[L], at(t - 3))
                        if v % 4 == 0:
                            loop_wait(dve, y_stored[v // 4][L], i * 16)
                        ts(y32[:, b:b + D], xs(t), one("rs2", t), one("nm2", t), ALU.mult, ALU.add).then_inc(y_ready[L], 1)
                        loop_wait(dve, y_ready[L], at(t + 1))
                        V.tensor_copy(y16[:, v * 512:v * 512 + D], y32[:, b:b + D]).then_inc(hi_ready[L], 1)
                        loop_wait(dve, hi_ready[L], at(t + 1))
                        tt(y16[:, v * 512 + D:(v + 1) * 512], y32[:, b:b + D], y16[:, v * 512:v * 512 + D], ALU.subtract).then_inc(yl_ready[L], 1)

                dve.wait_ge(logit_mm[L], at(TILES // 2))
                dve.wait_ge(yl_ready[L], at(TILES))
                dve.wait_ge(yT_ev[L], at(TILES // 2))
                if L == 0:
                    dve.wait_ge(x_plus_y[L], at(TILES))
                for h in range(2):
                    dve.wait_ge(y_stored[h][L], 16 * (TILES // 8))
                te = lambda a: a.rearrange("p (t e) -> p t e", e=E)
                et = lambda a: a.rearrange("p (e t) -> p e t", e=E)
                if L == 0:
                    ch.mark(V.tensor_copy(lg, bank[7][:]))
                else:
                    ch.mark(tt(te(lg), te(bank[7][:]), rows(gb_bc[:, 0:E], TILES), ALU.add))
                    ch.wait()
                    ch.mark(tt(te(lg), te(lg), rows(gb_bc[:, E:2 * E], TILES), ALU.add))
                ch.wait()
                for src, mx, M in ((lg, "m1", M1), (lg2, "m2", M2)):
                    ch.mark(V.tensor_reduce(col[mx], te(src), AX.X, ALU.max))
                    ch.wait()
                    ch.mark(tt(te(eqm), te(src), bc(col[mx], E), ALU.is_equal))
                    ch.wait()
                    ch.mark(tt(te(sc), te(eqm), rows(rank8[:], TILES), ALU.mult))
                    ch.wait()
                    ch.mark(V.tensor_reduce(col["rk"], te(sc), AX.X, ALU.max))
                    ch.wait()
                    ch.mark(tt(te(M), te(sc), bc(col["rk"], E), ALU.is_equal))
                    ch.wait()
                    if M is M1:
                        ch.mark(stt(lg2, M1, -3.0e38, lg, ALU.mult, ALU.add))
                        ch.wait()
                tt(col["tb"], col["m2"], col["m1"], ALU.subtract).then_inc(gap_ready[L], 1)
                tt(msum[:, 0:512], M1, M2, ALU.add).then_inc(msum_ready[L], 1)
                ch.mark(V.memset(onesd, 1.0))
                dve.wait_ge(rank_mm[L], at(1))
                ch.mark(V.tensor_copy(et(big_a), bank[1][:].rearrange("p (t e) -> p e t", e=E)))
                ch.wait()
                ch.mark(V.tensor_tensor_scan(big_b, onesd, big_a, 0.0, ALU.mult, ALU.add))
                ch.wait()
                ends, cnt, nt, tiles_to, base, adj_e, zero8 = (ex[:, 9 * k:9 * k + 9] for k in range(7))
                ch.mark(V.memset(ex[:], 0.0))
                ch.wait()
                ch.mark(V.tensor_copy(ends[:, 1:9].rearrange("p (e one) -> p e one", one=1), et(big_b)[:, :, TILES - 1:TILES]))
                ch.wait()
                ch.mark(tt(cnt[:, 0:E], ends[:, 1:9], ends[:, 0:8], ALU.subtract))
                ch.wait()
                ch.mark(ts(ex_i[:, 0:E], cnt[:, 0:E], float(P - 1), None, ALU.add))
                ch.wait()
                ch.mark(ts(ex_i[:, E:2 * E], ex_i[:, 0:E], 7, None, ALU.arith_shift_right))
                ch.wait()
                ch.mark(V.tensor_copy(nt[:, 0:E], ex_i[:, E:2 * E]))
                ch.wait()
                ch.mark(V.tensor_tensor_scan(tiles_to[:, 0:E], onesd[:, 0:E], nt[:, 0:E], 0.0, ALU.mult, ALU.add))
                ch.wait()
                ch.mark(tt(base[:, 0:E], tiles_to[:, 0:E], nt[:, 0:E], ALU.subtract))
                ch.wait()
                ch.mark(stt(adj_e[:, 0:E], base[:, 0:E], float(P), ends[:, 0:8], ALU.mult, ALU.subtract))
                ch.mark(tt(big_b, big_b, big_a, ALU.subtract))
                ch.wait()
                ch.mark(tt(et(big_b), et(big_b), bc(adj_e[:, 0:E], TILES), ALU.add))
                ch.wait()
                ch.mark(tt(pf.rearrange("p (t e) -> p e t", e=E), et(big_b), bank[0][:].rearrange("p (t e) -> p e t", e=E), ALU.add))
                ch.wait()
                for k, M in enumerate((M1, M2)):
                    ch.mark(tt(big_a, M, pf, ALU.mult))
                    ch.wait()
                    ch.mark(V.tensor_reduce(col["rk"], te(big_a), AX.X, ALU.add))
                    ch.wait()
                    ch.mark(V.tensor_copy(pos_i[k][:], col["rk"]))
                    ch.wait()
                    ch.mark(ts(tmp_i[:], pos_i[k][:], P - 1, None, ALU.bitwise_and))
                    ch.wait()
                    ch.mark(V.tensor_copy(col[f"lo{k}"], tmp_i[:]))
                    ch.wait()
                    ch.mark(ts(tmp_i[:], pos_i[k][:], 7, None, ALU.arith_shift_right))
                    ch.wait()
                    ch.mark(V.tensor_copy(col[f"hi{k}"], tmp_i[:]))
                    ch.wait()
                ch.mark(V.memset(inv_a[:, 0:P], 0.0))
                ch.wait()
                V.memset(inv_b[:, 0:SLOTS], 0.0).then_inc(ab_ready[L], 1)
                with dve.Fori(0, TILES // 2) as i:
                    ch.enter(i, 4)
                    for v in range(2):
                        for k in range(2):
                            b, t = 2 * v + k, 2 * i + v
                            loop_wait(dve, inv_mm[L], at(4 * i + b - 2))
                            if b == 0:
                                dve.wait_ge(inv_mm[L], at(1))
                            ch.mark(ts(inv_a[:, b * P:(b + 1) * P], iota_p[:], one(f"lo{k}", t), None, ALU.is_equal))
                            ts(inv_b[:, b * SLOTS:(b + 1) * SLOTS], iota_s[:], one(f"hi{k}", t), cut(token_id, t, 1),
                               ALU.is_equal, ALU.mult).then_inc(ab_ready[L], 1)
                ch.leave(TILES // 2)
                dve.wait_ge(inv_mm[L], at(2 * TILES + 1))
                ch.mark(V.memset(inv_a[:, 0:P], 0.0))
                ch.wait()
                V.memset(inv_b[:, 0:SLOTS], 0.0).then_inc(ab_ready[L], 1)
                ct = cmp_t[0:1, :].rearrange("p (s e) -> p s e", e=E)
                ch.mark(tt(ct, tiles_to[0:1, 0:E].rearrange("p (one e) -> p one e", one=1).to_broadcast([1, SLOTS, E]),
                           iota_s[0:1, :].rearrange("p (s one) -> p s one", one=1).to_broadcast([1, SLOTS, E]), ALU.is_le))
                ch.wait()
                ch.mark(V.tensor_reduce(big_a[0:1, 0:SLOTS], ct, AX.X, ALU.add))
                ch.wait()
                ch.mark(ts(slot_expert[:], big_a[0:1, 0:SLOTS], float(E - 1), None, ALU.min))
                dve.wait_ge(e2_ready[L], at(1))
                ch.mark(ts(col["tc"], col["ta"], 1.0, None, ALU.add))
                ch.wait()
                ch.mark(V.reciprocal(col["w1"], col["tc"]))
                ch.wait()
                ch.mark(tt(col["w2"], col["ta"], col["w1"], ALU.mult))
                ch.wait()
                dve.wait_ge(inv_mm[L], at(2 * TILES + 2))
                V.tensor_copy(slot_token[:], bank[2][:, 0:SLOTS]).then_inc(slots_ready[L], 1)

                def copy_T(s, u):
                    loop_wait(dve, T_mm[L], at(s + 1))
                    loop_wait(dve, h_mm[L], at(s - 3))
                    V.tensor_copy(tT[:, (u % SU) * 512:(u % SU + 1) * 512], bank[u % 2][:, 0:D].bitcast(F16)).then_inc(T_ev[L], 1)

                def cut_hidden(s, u):
                    loop_wait(dve, h_act[L], at(s + 1))
                    loop_wait(dve, o_mm[L], at(s - 1))
                    hb = (u % 2) * 512
                    ch.mark(V.tensor_copy(hid_hi[:, hb:hb + F], hid[:, hb:hb + F]))
                    ch.wait()
                    tt(hid_lo[:, hb:hb + F], hid[:, hb:hb + F], hid_hi[:, hb:hb + F], ALU.subtract).then_inc(h_split[L], 1)

                def experts(i, more):
                    for u in range(SU):
                        s = i * SU + u
                        if more or u + 2 < SU:
                            copy_T(s + 2, u + 2)
                        if more or u + 1 < SU:
                            cut_hidden(s + 1, u + 1)

                copy_T(0, 0)
                copy_T(1, 1)
                cut_hidden(0, 0)
                with dve.Fori(0, TURNS - 1) as i:
                    ch.enter(i, SU)
                    experts(i, True)
                ch.leave(TURNS - 1)
                experts(TURNS - 1, False)
            combine(dve, ch, 1, False)


_INS = ["x", "adj", "L0_gnn_W", "L0_gnn_a", "L0_ffn_router_w", "L0_ffn_w1", "L0_ffn_b1", "L0_ffn_w2", "L0_ffn_b2",
        "L1_gnn_W", "L1_gnn_a", "L1_ffn_Wg", "L1_ffn_bg", "L1_ffn_bias", "L1_ffn_W1", "L1_ffn_b1", "L1_ffn_W2", "L1_ffn_b2"]


def kernel(**inputs):
    import numpy as _np
    import concourse.bacc as _bacc
    from concourse import mybir as _mybir
    from concourse.bass_utils import run_bass_kernel_spmd as _run

    nc = _bacc.Bacc("TRN2", target_bir_lowering=False, num_devices=1)
    arrays, t = {}, {}
    for name in _INS:
        a = _np.ascontiguousarray(inputs[name])
        arrays[f"in_{name}"] = a
        t[name] = nc.dram_tensor(f"in_{name}", a.shape, _mybir.dt.from_np(a.dtype), kind="ExternalInput").ap()
    out = nc.dram_tensor("out_0", (GRAPHS, NODES, D), F32, kind="ExternalOutput").ap()
    build(nc, t["x"], t["adj"], (t["L0_gnn_W"], t["L1_gnn_W"]), (t["L0_gnn_a"], t["L1_gnn_a"]),
          (t["L0_ffn_router_w"], t["L1_ffn_Wg"]), t["L1_ffn_bg"], t["L1_ffn_bias"],
          (t["L0_ffn_w1"], t["L1_ffn_W1"]), (t["L0_ffn_b1"], t["L1_ffn_b1"]),
          (t["L0_ffn_w2"], t["L1_ffn_W2"]), (t["L0_ffn_b2"], t["L1_ffn_b2"]), out)
    r = _run(nc, [arrays], core_ids=[0])
    return r.results[0]["out_0"]
```

```python
import concourse.bass as bass
from concourse import mybir
from contextlib import ExitStack

F32 = mybir.dt.float32
F16 = mybir.dt.float16
I32 = mybir.dt.int32
U32 = mybir.dt.uint32
ALU = mybir.AluOpType
ACT = mybir.ActivationFunctionType
AX = mybir.AxisListType

P = 128
GRAPHS = 128
NODES = 64
D = 256
KC = D // P
TOKENS = GRAPHS * NODES
TILES = TOKENS // P
GT = 8
GROUPS = TILES // GT
E = 8
TOPK = 2
SLOT = 256
ST = SLOT // P
SLOTS = TOKENS * TOPK // SLOT + E
STILES = SLOTS * ST
SU = 4
SV = SU * ST
AHEAD_G = 12
HID = (256, 512)
NEG_BIG = -9000000000000000.0
EPS = 1e-5
LEAK = 0.2
WSCALE = 64.0
AHEAD = 16


def at(n):
    return n + AHEAD


def build(nc, x_in, adj, W_gnn, a_gnn, router, gate_b, gate_bias, w1, b1, w2, b2, out):
    ctx = ExitStack()
    with ctx:
        def sb(name, shape, dt=F32):
            return ctx.enter_context(nc.sbuf_tensor(name, shape, dt))

        def sem(name):
            return ctx.enter_context(nc.semaphore(name))

        def sem2(name):
            return [ctx.enter_context(nc.semaphore(f"{name}_{L}")) for L in range(2)]

        table = [nc.dram_tensor(f"split_tokens_{L}", (TOKENS, 2 * D), F16, kind="Internal").ap() for L in range(2)]
        ydram = [nc.dram_tensor(f"expert_outputs_{L}", (TOPK * TOKENS + STILES * P, D), F32, kind="Internal").ap() for L in range(2)]

        X = sb("X", [P, TILES * D])
        WREG = sb("WREG", [P, E * (8 * HID[1] + D)], F16)
        ident = sb("ident", [P, P])
        ident16 = sb("ident16", [P, P], F16)
        before16 = sb("before16", [P, P], F16)
        ones16 = sb("ones16", [P, P], F16)
        same_graph = sb("same_graph", [P, P])
        stacked_id = sb("stacked_id", [P, NODES])
        iota_p = sb("iota_p", [P, P], F16)
        iota_s = sb("iota_s", [P, STILES], F16)
        iota_sf = sb("iota_sf", [1, SLOTS])
        row_id = sb("row_id", [P, TOPK * TILES])
        part_id = sb("part_id", [P, 1])
        dump_id = sb("dump_id", [P, STILES])
        rank8 = sb("rank8", [P, E])
        eps_col = sb("eps_col", [P, 1])
        wg_sb = sb("wg_sb", [P, 2 * KC * D])
        a_cols = sb("a_cols", [P, 2 * 4])
        wgT = sb("wgT", [P, KC * D])
        rt_sb = sb("rt_sb", [P, 2 * KC * E])
        rt_rows = sb("rt_rows", [E, D])
        u_bc = sb("u_bc", [P, 2 * D])
        u_sum = sb("u_sum", [P, 2])
        gb_bc = sb("gb_bc", [P, 2 * E])
        b2_low64 = sb("b2_low64", [P, 1])
        b2_sign = sb("b2_sign", [P, 1])
        b1T = sb("b1T", [P, E * (HID[0] + HID[1]) // P])
        b2_pair = sb("b2_pair", [P, E * D], F16)
        b2_pick = sb("b2_pick", [P, 2 * P], F16)
        stats = sb("stats", [P, TILES * 6])
        cols = sb("cols", [P, 24 * TILES])
        names = ["mean", "rstd", "nmr", "s1", "s2", "dot1", "dot2", "ta", "tb", "tc", "w1", "w2",
                 "m1", "m2", "rk", "lo0", "hi0", "lo1", "hi1", "rs2", "nm2", "var", "sd", "td"]
        col = {n: cols[:, k * TILES:(k + 1) * TILES] for k, n in enumerate(names)}

        pos_i = [sb(f"pos_i{k}", [P, TILES], I32) for k in range(TOPK)]
        tmp_i = sb("tmp_i", [P, TILES], I32)
        gather_row = sb("gather_row", [P, STILES], U32)
        scatter_row = sb("scatter_row", [P, STILES], U32)
        slot_expert = sb("slot_expert", [1, SLOTS + SU], I32)
        slot_block = sb("slot_block", [1, SLOTS + SU], I32)
        ex = sb("ex", [P, 12 * 9])
        ex_i = sb("ex_i", [P, 2 * E], I32)
        gather_now = sb("gather_now", [P, SV], U32)
        scatter_now = sb("scatter_now", [P, SV], U32)
        rinv = sb("rinv", [P, 2 * GT])

        arena = sb("arena", [P, 9728])
        used = [0]

        def carve(n, start=None):
            if start is not None:
                used[0] = start
            a = arena[:, used[0]:used[0] + n]
            used[0] += n
            assert used[0] <= 9728
            return a

        adj_sb = carve(512, 0).bitcast(I32)
        neg = carve(512)
        diag = carve(512)
        scores = carve(512)
        probs = carve(GT * P)
        probsT = carve(GT * P)
        xn = carve(GT * D)
        gT = carve(2 * 2 * D)
        er_e = carve(4 * D)
        er_r = carve(4 * D)
        stage_w = sb("stage_w", [P, 2048])
        b2_rows = carve(E * D, 0)
        b2_hi = carve(E * D // 2).bitcast(F16)
        abc = carve(4 * P, 9216)
        comb = carve(2 * 8 * D, 0)
        junk = carve(4 * D)
        y32 = carve(4 * D, 0)
        y16 = carve(8 * D).bitcast(F16)
        yT = carve(2 * 2 * D)
        lg, eqm, sc, M1, M2, lg2, pf, big_a, big_b, onesd = (carve(512, 0 if k == 0 else None) for k in range(10))
        cmp_t = carve(SLOTS * E)
        msum = carve(256).bitcast(F16)
        inv_a = carve(8 * P // 2).bitcast(F16)
        inv_b = carve(8 * STILES).bitcast(F16)
        inv_v, inv_w, inv_x = (carve(STILES) for _ in range(3))
        inv_i = carve(STILES).bitcast(I32)
        gat = carve(SV * D, 0).bitcast(F16)
        tT = carve(2 * 2 * SLOT).bitcast(F16)
        hid = carve(2 * 4 * SLOT)
        hid_hi = carve(4 * SLOT).bitcast(F16)
        hid_lo = carve(4 * SLOT).bitcast(F16)
        o_sb = carve(SV * D)

        bank = [ctx.enter_context(nc.psum_tensor(f"bank{k}", [P, 512], F32)) for k in range(8)]

        go = sem("go")
        pool_tick = sem("pool_tick")
        const_pool = sem("const_pool")
        const_ready = sem("const_ready")
        small_in = sem("small_in")
        b2_in = sem("b2_in")
        setup_dve = sem("setup_dve")
        setup_mm = sem("setup_mm")
        x_loaded = [sem(f"x_loaded_{k}") for k in range(4)]
        adj_loaded, out_stored = sem2("adj_loaded"), sem("out_stored")
        weights_loaded = [sem2(f"weights_loaded_{k}") for k in range(2)]
        y_stored = [sem2(f"y_stored_{k}") for k in range(2)]
        gathered = [sem(f"gathered_{k}") for k in range(SU)]
        scattered = [sem(f"scattered_{k}") for k in range(SV)]
        c_loaded = [sem(f"c_loaded_{k}") for k in range(2)]
        own = sem("dve_own")
        neg_ready, diag_ready, scaled, split_done, x_plus_y, idx_ready, sidx_ready = by_pool = [sem2(n) for n in (
            "neg_ready", "diag_ready", "scaled", "split_done", "x_plus_y", "idx_ready", "sidx_ready")]
        E_mm, PT_mm, G_mm, H_mm, yT_mm, logit_mm, rank_mm, inv_mm, T_mm, h_mm, o_mm = by_pe = [sem2(n) for n in (
            "E_mm", "PT_mm", "G_mm", "H_mm", "yT_mm", "logit_mm", "rank_mm", "inv_mm", "T_mm", "h_mm", "o_mm")]
        E_ev, exp_done, PT_ev, G_ev, e_done, ER_done, yT_ev, sd_ready, e2_ready, h_act, o_ev = by_act = [sem2(n) for n in (
            "E_ev", "exp_done", "PT_ev", "G_ev", "e_done", "ER_done", "yT_ev", "sd_ready", "e2_ready", "h_act", "o_ev")]
        (combined, var_ready, s_ready, sm_ready, xn_ready, post, rinv_ready, y_ready, hi_ready, yl_ready, gap_ready,
         msum_ready, ab_ready, slots_ready, T_ev, h_split) = by_dve = [sem2(n) for n in (
            "combined", "var_ready", "s_ready", "sm_ready", "xn_ready", "post", "rinv_ready", "y_ready", "hi_ready",
            "yl_ready", "gap_ready", "msum_ready", "ab_ready", "slots_ready", "T_ev", "h_split")]

        def credit(eng, sems):
            for pair in sems:
                for s in pair:
                    eng.sem_inc(s, AHEAD)

        def loop_wait(eng, s, value):
            eng.wait_ge(s, value)
            eng.wait_ge(go, 1)

        def used_before(L, i):
            return L > 0 or not isinstance(i, int) or i > 0

        class Chain:

            def __init__(self, eng, s):
                self.eng, self.s, self.n, self.base = eng, s, 0, 0

            def mark(self, ins):
                ins.then_inc(self.s, 1)
                self.n += 1
                return self.n

            def wait(self, n=None):
                loop_wait(self.eng, self.s, self.base + (self.n if n is None else n))

            def enter(self, i, per_turn):
                self.base, self.start, self.per = i * per_turn, self.n, per_turn

            def leave(self, turns):
                assert self.n - self.start == self.per, (self.n - self.start, self.per)
                self.base, self.n = 0, self.start + self.per * turns

        block = ctx.enter_context(nc.Block())

        xt_dram = x_in.rearrange("(t two) n d -> (two n) t d", two=2)
        out_dram = out.rearrange("(t two) n d -> (two n) t d", two=2)
        adj_dram = adj.rearrange("(t two) i j -> (two i) t j", two=2)
        TURNS = SLOTS // SU

        def cut(a, start, n):
            return a[:, start:start + n] if isinstance(start, int) else a[:, bass.ds(start, n)]

        def cut3(a, start, n):
            return a[:, start:start + n, :] if isinstance(start, int) else a[:, bass.ds(start, n), :]

        def xs(t, n=1):
            return cut(X, t * D, n * D)

        def one(name, t, n=1):
            return cut(cols, names.index(name) * TILES + t, n)

        def bc(a, n):
            return a.rearrange("p (m one) -> p m one", one=1).to_broadcast([P, a.shape[1], n])

        def rows(a, n):
            return a.rearrange("p (one m) -> p one m", one=1).to_broadcast([P, n, a.shape[1]])

        def w1_at(L, e, hl, kc, fc):
            return cut(WREG, e + ((hl * KC + kc) * HID[L] + fc * P), P)

        def w2_at(L, e, hl, fc):
            return cut(WREG, e + (4 * HID[L] + (hl * (HID[L] // P) + fc) * D), D)

        slot_regs = {}

        def of_slots(eng, table, i, n, per):
            if table.name not in slot_regs:
                slot_regs[table.name] = [eng.alloc_register(f"{table.name}_{k}") for k in range(SU + 2)]
            eng.reg_load(slot_regs[table.name][:n], cut(table, i * SU, n))
            return [eng.snap(r, min_val=0, max_val=(E - 1) * per) for r in slot_regs[table.name][:n]]

        def load_outputs(sp, L):
            for u in range(SV):
                sp.wait_ge(scattered[u], 16 * TURNS * (L + 1))
            with sp.Fori(0, TILES // 8) as i:
                for h in range(2):
                    sp.wait_ge(combined[L], at(i * 8 + 4 * h - 4))
                    for k in range(TOPK):
                        sp.dma_start(comb[:, (8 * h + 4 * k) * D:(8 * h + 4 * k + 4) * D].rearrange("p (t d) -> p t d", d=D),
                                     ydram[L][0:TOPK * TOKENS, :].rearrange("(t p) d -> p t d", p=P)[:, bass.ds(i * 8 + (4 * h + TILES * k), 4), :]
                                     ).then_inc(c_loaded[h], 16)

        def combine(dve, ch, L, stats_too):
            V = nc.vector

            def add(k, t, u):
                return V.scalar_tensor_tensor(xs(t), comb[:, (8 * (u // 4) + 4 * k + u % 4) * D:(8 * (u // 4) + 4 * k + u % 4 + 1) * D],
                                              one(f"w{k + 1}", t), xs(t), ALU.mult, ALU.add)

            with dve.Fori(0, TILES // 8) as i:
                ch.enter(i, 8 * (1 + (3 if stats_too else 0)))
                for u in range(8 + 1):
                    t = i * 8 + u
                    if u < 8:
                        if u % 4 == 0:
                            loop_wait(dve, c_loaded[u // 4], 32 * (TILES // 8) * L + i * 32 + 32)
                        first = ch.mark(add(0, t, u))
                    if stats_too and u:
                        loop_wait(dve, combined[L], at(t))
                        ch.mark(V.bn_stats(cut(stats, (t - 1) * 6, 6), xs(t - 1)))
                        dots(ch, t - 1, (u - 1) % 2)
                    if u < 8:
                        ch.wait(first)
                        add(1, t, u).then_inc(combined[L], 1)
            ch.leave(TILES // 8)

        def dots(ch, t, h):
            for j in range(2):
                ch.wait(ch.n - 3)
                ch.mark(nc.vector.scalar_tensor_tensor(junk[:, (2 * h + j) * D:(2 * h + j + 1) * D], xs(t), 1.0, u_bc[:, j * D:(j + 1) * D],
                                                       ALU.mult, ALU.mult, accum_out=one(f"dot{j + 1}", t)))

        @block.sync
        def _(sp):
            sp.sem_inc(go, 1)
            for L in range(2):
                for h in range(2):
                    sp.sem_inc(y_stored[h][L], 16)
            for L in range(2):
                sp.dma_start(wg_sb[:, L * KC * D:(L + 1) * KC * D].rearrange("p (k n) -> p k n", k=KC),
                             W_gnn[L].rearrange("(k p) n -> p k n", p=P)).then_inc(small_in, 16)
                with nc.allow_non_contiguous_dma(reason="vectors onto partitions"):
                    sp.dma_start(a_cols[:, L * 4:(L + 1) * 4],
                                 a_gnn[L].rearrange("(k p) one -> p (k one)", p=P)).then_inc(small_in, 16)
                    base = L * E * HID[0] // P
                    sp.dma_start(b1T[:, base:base + E * HID[L] // P].rearrange("p (e c) -> p e c", e=E),
                                 b1[L].rearrange("e (c p) -> p e c", p=P)).then_inc(small_in, 16)
            sp.dma_start(rt_rows[:], router[0]).then_inc(small_in, 16)
            sp.dma_start(rt_sb[:, KC * E:2 * KC * E].rearrange("p (k n) -> p k n", k=KC),
                         router[1].rearrange("(k p) n -> p k n", p=P)).then_inc(small_in, 16)
            for k, v in enumerate((gate_b, gate_bias)):
                sp.dma_start(gb_bc[:, k * E:(k + 1) * E],
                             v.rearrange("(one e) -> one e", one=1).to_broadcast([P, E])).then_inc(small_in, 16)
            sp.wait_ge(const_ready, 1)
            for k in range(4):
                sp.dma_start(b2_rows[32 * k:32 * k + 1, :],
                             b2[k // 2].rearrange("(one e) d -> one (e d)", one=1)).then_inc(b2_in, 16)
            for c in range(TILES // 4):
                if c >= 4:
                    sp.wait_ge(x_loaded[c % 4], 16 * (c // 4))
                sp.dma_start(xs(4 * c, 4).rearrange("p (t d) -> p t d", d=D),
                             xt_dram[:, 4 * c:4 * c + 4, :]).then_inc(x_loaded[c % 4], 16)

            for L in range(2):
                F = HID[L]
                if L == 0:
                    sp.wait_ge(s_ready[0], at(1))
                else:
                    sp.wait_ge(s_ready[1], at(1))
                def load_weights(e, k):
                    n = F // P if k else KC
                    src = w2[L].rearrange("e (k p) n -> p (e k) n", p=P) if k else w1[L].rearrange("e (k p) f -> p (e k) f", p=P)
                    sp.wait_ge(split_done[L], at(2 * e + k - 1))
                    sp.dma_start(stage_w[:, 2 * F * k:2 * F * (k + 1)].rearrange("p (k f) -> p k f", k=n),
                                 cut3(src, e * n, n)).then_inc(weights_loaded[k][L], 16)

                with sp.Fori(0, GROUPS // 2) as g:
                    for k in range(2):
                        sp.wait_ge(neg_ready[L], at(2 * g + k))
                        sp.dma_start(adj_sb.rearrange("p (t j) -> p t j", t=GT),
                                     adj_dram[:, bass.ds(g * (2 * GT) + k * GT, GT), :]).then_inc(adj_loaded[L], 16)
                        load_weights(g, k)
                for k in range(2):
                    load_weights(E // 2, k)
                with sp.Fori(0, TILES // 8) as i:
                    for h in range(2):
                        sp.wait_ge(yl_ready[L], at(i * 8 + 4 * h + 4))
                        sp.dma_start(table[L].rearrange("(t p) c -> p t c", p=P)[:, bass.ds(i * 8 + 4 * h, 4), :],
                                     y16[:, 4 * h * 512:(4 * h + 4) * 512].rearrange("p (t c) -> p t c", t=4)).then_inc(y_stored[h][L], 16)
                with sp.Fori(E // 2 + 1, E) as e:
                    for k in range(2):
                        load_weights(e, k)
                load_outputs(sp, L)
            with sp.Fori(0, TILES // 4) as i:
                sp.wait_ge(combined[1], at(i * 4 + 4))
                sp.dma_start(out_dram[:, bass.ds(i * 4, 4), :], xs(i * 4, 4).rearrange("p (t d) -> p t d", d=D)).then_inc(out_stored, 16)
            sp.wait_ge(out_stored, 16 * (TILES // 4))

        @block.gpsimd
        def _(pool):
            credit(pool, by_pool)
            n = 0

            def step(ins):
                nonlocal n
                n += 1
                ins.then_inc(const_pool, 1)
                pool.wait_ge(const_pool, n)

            for t_, v in ((ident, 0.0), (ident16, 0.0), (before16, 1.0), (same_graph, 0.0), (stacked_id, 0.0),
                          (ones16, 1.0), (eps_col, EPS), (b2_pick, 0.0), (b2_low64, 0.0), (b2_sign, 1.0)):
                step(nc.gpsimd.memset(t_[:], v))
            step(nc.gpsimd.memset(b2_rows, 0.0))
            for t_ in (ident, ident16):
                step(nc.gpsimd.affine_select(out=t_[:], in_=t_[:], compare_op=ALU.not_equal, fill=1.0, base=0,
                                             pattern=[[-1, P]], channel_multiplier=1))
            step(nc.gpsimd.affine_select(out=before16[:], in_=before16[:], compare_op=ALU.is_gt, fill=0.0, base=0,
                                         pattern=[[1, P]], channel_multiplier=-1))
            step(nc.gpsimd.memset(same_graph[0:NODES, 0:NODES], 1.0))
            step(nc.gpsimd.memset(same_graph[NODES:P, NODES:P], 1.0))
            for k in range(4):
                step(nc.gpsimd.memset(b2_pick[32 * k:32 * k + 1, (k // 2) * P:(k // 2 + 1) * P], 1.0))
                if k % 2:
                    step(nc.gpsimd.memset(b2_low64[32 * k:32 * k + 1, :], WSCALE))
                    step(nc.gpsimd.memset(b2_sign[32 * k:32 * k + 1, :], -1.0))
            for b in (0, NODES):
                step(nc.gpsimd.affine_select(out=stacked_id[:], in_=stacked_id[:], compare_op=ALU.not_equal, fill=1.0,
                                             base=-b, pattern=[[-1, NODES]], channel_multiplier=1))
            for t_, pat, base, cm in ((iota_p[:], [[1, P]], 0, 0), (iota_s[:], [[1, STILES]], 0, 0),
                                      (iota_sf[:], [[1, SLOTS]], 0, 0), (row_id[:], [[1, TOPK * TILES]], 0, 0),
                                      (part_id[:], [[1, 1]], 1, 1), (dump_id[:], [[P, STILES]], TOPK * TOKENS + 1, 1),
                                      (rank8[:], [[-1, E]], E, 0)):
                step(nc.gpsimd.iota(t_, pattern=pat, base=base, channel_multiplier=cm,
                                    allow_small_or_imprecise_dtypes=True))
            nc.gpsimd.memset(gather_now[:], 0).then_inc(const_ready, 1)

            for L in range(2):
                F = HID[L]
                def cut_weights(e, k):
                    stage = stage_w[:, 2 * F * k:2 * F * (k + 1)]
                    hi, lo = (cut(WREG, e * (8 * F + D) + (4 * F * k + 2 * F * h), 2 * F) for h in range(2))
                    pool.wait_ge(weights_loaded[k][L], e * 16 + 16)
                    pool.sem_inc(pool_tick)
                    nc.gpsimd.tensor_scalar(stage, stage, WSCALE, None, ALU.mult).then_inc(scaled[L], 1)
                    loop_wait(pool, scaled[L], at(e * 4 + 2 * k + 1))
                    nc.gpsimd.tensor_copy(hi, stage).then_inc(scaled[L], 1)
                    if k:
                        nc.gpsimd.tensor_copy(cut(WREG, e * (8 * F + D) + 8 * F, D), cut(b2_pair, e * D, D))
                    loop_wait(pool, scaled[L], at(e * 4 + 2 * k + 2))
                    nc.gpsimd.tensor_tensor(lo, stage, hi, ALU.subtract).then_inc(split_done[L], 1)

                pool.wait_ge(setup_dve, 1)
                with pool.Fori(0, GROUPS // 2) as i:
                    for k in range(2):
                        g = 2 * i + k
                        pool.wait_ge(sm_ready[L], at(g))
                        pool.wait_ge(adj_loaded[L], g * 16 + 16)
                        pool.sem_inc(pool_tick)
                        nc.gpsimd.tensor_scalar(neg, adj_sb, 0, NEG_BIG, ALU.is_le, ALU.mult).then_inc(neg_ready[L], 1)
                        pool.wait_ge(s_ready[L], at(1))
                        loop_wait(pool, E_mm[L], at(g))
                        nc.gpsimd.tensor_tensor(diag.rearrange("p (t j) -> p t j", t=GT), rows(stacked_id[:], GT),
                                                bc(one("s2", g * GT, GT), NODES), ALU.mult).then_inc(diag_ready[L], 1)
                        cut_weights(i, k)
                if L == 0:
                    with pool.Fori(0, TILES // 4) as i:
                        for u in range(4):
                            loop_wait(pool, y_ready[L], at(i * 4 + u + 1))
                            nc.gpsimd.tensor_tensor(xs(i * 4 + u), xs(i * 4 + u), y32[:, u * D:(u + 1) * D],
                                                    ALU.add).then_inc(x_plus_y[L], 1)
                with pool.Fori(E // 2, E) as e:
                    for k in range(2):
                        cut_weights(e, k)
                for h in range(2):
                    pool.wait_ge(y_stored[h][L], 16 + 16 * (TILES // 8))
                pool.wait_ge(slots_ready[L], at(1))
                def gather(i, u, t):
                    if u % 4 == 0:
                        loop_wait(pool, T_mm[L], at((i - 1) * SU + u // 2 + 2))
                        nc.gpsimd.tensor_copy(gather_now[:, u:u + 4], cut(gather_row, t, 4)).then_inc(idx_ready[L], 1)
                        pool.wait_ge(idx_ready[L], at(i * 2 + u // 4 + 1))
                        pool.sem_inc(pool_tick)
                    nc.gpsimd.indirect_dma_start(
                        out=gat[:, u * 512:(u + 1) * 512], out_offset=None, in_=table[L],
                        in_offset=bass.IndirectOffsetOnAxis(ap=gather_now[:, u:u + 1], axis=0)).then_inc(gathered[u // ST], 16)

                def scatter(i, u, t):
                    if u % 4 == 0:
                        for v in range(4):
                            if used_before(L, i):
                                loop_wait(pool, scattered[u + v], 16 * TURNS * L + 16 * i)
                        nc.gpsimd.tensor_copy(scatter_now[:, u:u + 4], cut(scatter_row, t, 4)).then_inc(sidx_ready[L], 1)
                        pool.wait_ge(sidx_ready[L], at(i * 2 + u // 4 + 1))
                    if u % ST == 0:
                        pool.wait_ge(o_ev[L], at(i * SU + u // ST + 1))
                        pool.sem_inc(pool_tick)
                    nc.gpsimd.indirect_dma_start(
                        out=ydram[L], out_offset=bass.IndirectOffsetOnAxis(ap=scatter_now[:, u:u + 1], axis=0),
                        in_=o_sb[:, u * D:(u + 1) * D], in_offset=None).then_inc(scattered[u], 16)

                def move(i, left):
                    for u in range(SV):
                        t = i * SV + u
                        if u + AHEAD_G < (left + 1) * SV:
                            gather(i + (u + AHEAD_G) // SV, (u + AHEAD_G) % SV, t + AHEAD_G)
                        scatter(i, u, t)

                for t in range(AHEAD_G):
                    gather(t // SV, t % SV, t)
                move(0, 2)
                with pool.Fori(1, TURNS - 2) as i:
                    move(i, 2)
                move(TURNS - 2, 1)
                move(TURNS - 1, 0)

        @block.tensor
        def _(pe):
            credit(pe, by_pe)
            mm = nc.tensor.matmul
            pe.wait_ge(const_ready, 1)
            pe.wait_ge(small_in, 16 * 10)
            for c in range(KC):
                last = nc.tensor.transpose(bank[2][:, c * E:(c + 1) * E], rt_rows[:, c * P:(c + 1) * P], ident[0:E, 0:E])
            last.then_inc(setup_mm, 1)

            def edge_vectors(L):
                for oc in range(KC):
                    for fc in range(KC):
                        last = nc.tensor.transpose(bank[0][:, oc * D + fc * P:oc * D + (fc + 1) * P],
                                                   wg_sb[:, (L * KC + fc) * D + oc * P:(L * KC + fc) * D + (oc + 1) * P], ident[:])
                last.then_inc(setup_mm, 1)
                pe.wait_ge(setup_dve, 2 + 2 * L + 1)
                for j in range(2):
                    for oc in range(KC):
                        last = mm(bank[1][:, j * D:(j + 1) * D], abc[:, (2 * j + oc) * P:(2 * j + oc + 1) * P],
                                  wgT[:, oc * D:(oc + 1) * D], start=oc == 0, stop=oc == KC - 1)
                last.then_inc(setup_mm, 1)

            def scores_of(L, g):
                loop_wait(pe, diag_ready[L], at(g + 1))
                loop_wait(pe, E_ev[L], at(g))
                mm(bank[0][:], same_graph[:], diag[:], start=True, stop=False)
                mm(bank[0][:].rearrange("p (t j) -> p t j", t=GT), ident[:], bc(one("s1", g * GT, GT), NODES),
                   start=False, stop=True).then_inc(E_mm[L], 1)

            def attend(L, g, more):
                if more:
                    scores_of(L, g + 1)
                for h in range(2):
                    if h == 0:
                        loop_wait(pe, exp_done[L], at(g + 1))
                    loop_wait(pe, PT_ev[L], at(2 * g + h - 1))
                    for j in range(4):
                        last = nc.tensor.transpose(bank[1 + h][:, j * P:(j + 1) * P],
                                                   probs[:, (4 * h + j) * P:(4 * h + j + 1) * P], ident[:])
                    last.then_inc(PT_mm[L], 1)

                def aggregate(q):
                    if q == 0:
                        loop_wait(pe, xn_ready[L], at(g + 1))
                    if q % 2 == 0:
                        loop_wait(pe, PT_ev[L], at(2 * g + q // 2 + 1))
                    loop_wait(pe, G_ev[L], at(4 * g + q - 1))
                    for a in range(2):
                        for c in range(KC):
                            j = 2 * q + a
                            last = mm(bank[3 + q % 2][:, (2 * a + c) * P:(2 * a + c + 1) * P],
                                      xn[:, j * D + c * P:j * D + (c + 1) * P], probsT[:, j * P:(j + 1) * P],
                                      start=True, stop=True)
                    last.then_inc(G_mm[L], 1)

                def project(q):
                    loop_wait(pe, G_ev[L], at(4 * g + q + 1))
                    loop_wait(pe, ER_done[L], at(8 * g + 2 * q - 2))
                    for a in range(2):
                        for c in range(KC):
                            o = (q % 2) * 2 * D + a * D + c * P
                            last = mm(bank[5 + q % 2][:, a * D:(a + 1) * D], gT[:, o:o + P],
                                      wg_sb[:, (L * KC + c) * D:(L * KC + c + 1) * D], start=c == 0, stop=c == KC - 1)
                    last.then_inc(H_mm[L], 1)

                aggregate(0)
                aggregate(1)
                project(0)
                aggregate(2)
                project(1)
                aggregate(3)
                project(2)
                project(3)

            for L in range(2):
                F = HID[L]
                FC = F // P
                edge_vectors(L)
                scores_of(L, 0)
                with pe.Fori(0, GROUPS - 1) as g:
                    attend(L, g, True)
                attend(L, GROUPS - 1, False)

                with pe.Fori(0, TILES // 4) as i:
                    for q in range(2):
                        loop_wait(pe, y_ready[L], at(4 * i + 2 * q + 2))
                        loop_wait(pe, yT_ev[L], at(2 * i + q - 1))
                        for a in range(2):
                            for c in range(KC):
                                last = nc.tensor.transpose(bank[q][:, (2 * a + c) * P:(2 * a + c + 1) * P],
                                                           y32[:, (2 * q + a) * D + c * P:(2 * q + a) * D + (c + 1) * P], ident[:])
                        last.then_inc(yT_mm[L], 1)
                    for q in range(2):
                        loop_wait(pe, yT_ev[L], at(2 * i + q + 1))
                        for a in range(2):
                            for c in range(KC):
                                last = mm(bank[7][:, bass.ds((4 * i + 2 * q + a) * E, E)],
                                          yT[:, q * 2 * D + (2 * a + c) * P:q * 2 * D + (2 * a + c + 1) * P],
                                          rt_sb[:, (L * KC + c) * E:(L * KC + c + 1) * E], start=c == 0, stop=c == KC - 1)
                        last.then_inc(logit_mm[L], 1)

                pe.wait_ge(msum_ready[L], at(1))
                mm(bank[0][:], before16[:], msum[:, 0:512], start=True, stop=True)
                mm(bank[1][:], ones16[:], msum[:, 0:512], start=True, stop=True).then_inc(rank_mm[L], 1)
                pe.wait_ge(ab_ready[L], at(1))
                inv = bank[2][:, 0:2 * STILES]
                mm(inv, inv_a[:, 0:P], inv_b[:, 0:2 * STILES], start=True, stop=False).then_inc(inv_mm[L], 1)
                with pe.Fori(0, TILES // 4) as i:
                    for b in range(8):
                        pe.wait_ge(ab_ready[L], at(8 * i + b + 2))
                        mm(inv, inv_a[:, b * P:(b + 1) * P], inv_b[:, 2 * b * STILES:2 * (b + 1) * STILES],
                           start=False, stop=False).then_inc(inv_mm[L], 1)
                pe.wait_ge(ab_ready[L], at(2 * TILES + 2))
                mm(inv, inv_a[:, 0:P], inv_b[:, 0:2 * STILES], start=False, stop=True).then_inc(inv_mm[L], 1)

                def turn_over(i, s, u):
                    pe.wait_ge(gathered[u % SU], 16 * ST * (TURNS * L + i + u // SU + 1))
                    for j in range(4):
                        for a in range(ST):
                            q = (u % SU) * ST + a
                            last = nc.tensor.transpose(bank[u % 2][:, (j * ST + a) * (P // 2):(j * ST + a + 1) * (P // 2)].bitcast(F16),
                                                       gat[:, q * 512 + j * P:q * 512 + (j + 1) * P], ident16[:])
                    last.then_inc(T_mm[L], 1)

                def hidden(s, u, e):
                    loop_wait(pe, T_ev[L], at(s + 1))
                    for fc in range(FC):
                        n = 0
                        hb = bank[2 + 2 * (u % 2) + fc // 2][:, (fc % 2) * SLOT:(fc % 2 + 1) * SLOT]
                        for kc in range(KC):
                            for wh, yh in ((0, 0), (0, 1), (1, 0)):
                                tb = ((u % 2) * 4 + yh * KC + kc) * SLOT
                                last = mm(hb, w1_at(L, e, wh, kc, fc), tT[:, tb:tb + SLOT], start=n == 0, stop=n == 3 * KC - 1)
                                n += 1
                    last.then_inc(h_mm[L], 1)

                def output(s, u, e):
                    pe.wait_ge(h_split[L], at(s + 1))
                    loop_wait(pe, o_ev[L], at(s - 1))
                    ob = [bank[6 + u % 2][:, a * D:(a + 1) * D] for a in range(ST)]
                    hb = (u % 2) * 4 * SLOT
                    for a in range(ST):
                        for fc in range(FC):
                            for n, (hsrc, wh) in enumerate(((hid_hi, 0), (hid_lo, 0), (hid_hi, 1))):
                                h0 = hb + fc * SLOT + a * P
                                mm(ob[a], hsrc[:, h0:h0 + P], w2_at(L, e, wh, fc), start=fc == 0 and n == 0, stop=False)
                        last = mm(ob[a], b2_pick[:, L * P:(L + 1) * P], cut(WREG, e + 8 * F, D), start=False, stop=True)
                    last.then_inc(o_mm[L], 1)

                def experts(i, more):
                    es = of_slots(pe, slot_block, i, SU + (2 if more else 0), 8 * F + D)
                    for u in range(SU):
                        s = i * SU + u
                        output(s, u, es[u])
                        if more or u + 3 < SU:
                            turn_over(i, s + 3, u + 3)
                        if more or u + 2 < SU:
                            hidden(s + 2, u + 2, es[u + 2])

                pe.wait_ge(slots_ready[L], at(1))
                first = of_slots(pe, slot_block, 0, 2, 8 * F + D)
                for s in range(2):
                    turn_over(0, s, s)
                hidden(0, 0, first[0])
                turn_over(0, 2, 2)
                hidden(1, 1, first[1])
                with pe.Fori(0, TURNS - 1) as i:
                    experts(i, True)
                experts(TURNS - 1, False)

        @block.scalar
        def _(act):
            credit(act, by_act)
            A = nc.scalar.activation

            def copy_scores(L, g):
                loop_wait(act, E_mm[L], at(g + 1))
                loop_wait(act, exp_done[L], at(g))
                A(scores, bank[0][:], ACT.Copy).then_inc(E_ev[L], 1)

            def exponent(L, g):
                loop_wait(act, sm_ready[L], at(g + 1))
                loop_wait(act, PT_mm[L], at(2 * g))
                loop_wait(act, rinv_ready[L], at(g))
                for r in range(2):
                    pr = slice(r * NODES, (r + 1) * NODES)
                    ins = A(probs.rearrange("p (t c) -> p t c", t=GT)[pr, :, r * NODES:(r + 1) * NODES],
                            scores.rearrange("p (t j) -> p t j", t=GT)[pr, :, :], ACT.Exp)
                ins.then_inc(exp_done[L], 1)

            def attend(L, g, more):
                if more:
                    copy_scores(L, g + 1)
                for h in range(2):
                    loop_wait(act, PT_mm[L], at(2 * g + h + 1))
                    loop_wait(act, G_mm[L], at(4 * g))
                    A(probsT[:, h * 512:(h + 1) * 512], bank[1 + h][:], ACT.Copy).then_inc(PT_ev[L], 1)

                def copy_g(q):
                    loop_wait(act, G_mm[L], at(4 * g + q + 1))
                    loop_wait(act, H_mm[L], at(4 * g + q - 1))
                    A(gT[:, (q % 2) * 512:(q % 2 + 1) * 512], bank[3 + q % 2][:], ACT.Copy).then_inc(G_ev[L], 1)

                def elu_parts(q):
                    for a in range(2):
                        j = 2 * q + a
                        if a == 0:
                            loop_wait(act, H_mm[L], at(4 * g + q + 1))
                            if q == 0:
                                loop_wait(act, rinv_ready[L], at(g + 1))
                        loop_wait(act, post[L], at(8 * g + j - 3))
                        src = bank[5 + q % 2][:, a * D:(a + 1) * D]
                        b = (j % 4) * D
                        A(er_e[:, b:b + D], src, ACT.Exp, scale=rinv[:, j:j + 1]).then_inc(e_done[L], 1)
                        A(er_r[:, b:b + D], src, ACT.Relu, scale=rinv[:, j:j + 1]).then_inc(ER_done[L], 1)

                copy_g(0)
                copy_g(1)
                elu_parts(0)
                copy_g(2)
                elu_parts(1)
                if more:
                    exponent(L, g + 1)
                copy_g(3)
                elu_parts(2)
                elu_parts(3)

            for L in range(2):
                F = HID[L]
                FC = F // P
                act.wait_ge(var_ready[L], at(1))
                A(col["sd"], col["var"], ACT.Sqrt, bias=eps_col[:]).then_inc(sd_ready[L], 1)
                copy_scores(L, 0)
                exponent(L, 0)
                with act.Fori(0, GROUPS - 1) as g:
                    attend(L, g, True)
                attend(L, GROUPS - 1, False)
                act.wait_ge(var_ready[L], at(2))
                A(col["sd"], col["var"], ACT.Sqrt, bias=eps_col[:]).then_inc(sd_ready[L], 1)
                with act.Fori(0, TILES // 4) as i:
                    for q in range(2):
                        loop_wait(act, yT_mm[L], at(2 * i + q + 1))
                        loop_wait(act, logit_mm[L], at(2 * i + q - 1))
                        A(yT[:, q * 512:(q + 1) * 512], bank[q][:], ACT.Copy).then_inc(yT_ev[L], 1)
                act.wait_ge(gap_ready[L], at(1))
                A(col["ta"], col["tb"], ACT.Exp).then_inc(e2_ready[L], 1)

                def activate(s, u, e):
                    loop_wait(act, h_mm[L], at(s + 1))
                    loop_wait(act, h_split[L], at(s - 1))
                    base = L * E * HID[0] // P
                    for fc in range(FC):
                        h0 = ((u % 2) * 4 + fc) * SLOT
                        ins = A(hid[:, h0:h0 + SLOT], bank[2 + 2 * (u % 2) + fc // 2][:, (fc % 2) * SLOT:(fc % 2 + 1) * SLOT],
                                ACT.Gelu if L == 0 else ACT.Relu, bias=cut(b1T, e * FC + (base + fc), 1), scale=1.0 / WSCALE)
                    ins.then_inc(h_act[L], 1)

                def copy_out(s, u, i):
                    loop_wait(act, o_mm[L], at(s + 1))
                    if used_before(L, i):
                        for a in range(ST):
                            loop_wait(act, scattered[u * ST + a], 16 * TURNS * L + 16 * i)
                    A(o_sb[:, u * ST * D:(u + 1) * ST * D], bank[6 + u % 2][:, 0:ST * D], ACT.Copy, scale=1.0 / WSCALE).then_inc(o_ev[L], 1)

                def experts(i, more):
                    es = of_slots(act, slot_expert, i, SU + (2 if more else 0), 1)
                    for u in range(SU):
                        s = i * SU + u
                        if more or u + 2 < SU:
                            activate(s + 2, u + 2, es[u + 2])
                        copy_out(s, u, i)

                act.wait_ge(slots_ready[L], at(1))
                first = of_slots(act, slot_expert, 0, 2, 1)
                for s in range(2):
                    activate(s, s, first[s])
                experts(0, True)
                with act.Fori(1, TURNS - 1) as i:
                    experts(i, True)
                experts(TURNS - 1, False)

        @block.vector
        def _(dve):
            credit(dve, by_dve)
            V = nc.vector
            ch = Chain(dve, own)
            tt, stt, ts = V.tensor_tensor, V.scalar_tensor_tensor, V.tensor_scalar
            stats3 = stats[:].rearrange("p (t s) -> p t s", s=6)

            def st(k):
                return stats3[:, :, k:k + 1].rearrange("p t one -> p (t one)")

            dve.wait_ge(const_ready, 1)
            dve.wait_ge(b2_in, 64)
            ch.mark(ts(b2_hi, b2_rows, WSCALE, None, ALU.mult))
            ch.wait()
            ch.mark(ts(b2_rows, b2_rows, b2_low64[:], None, ALU.mult))
            ch.wait()
            stt(b2_pair[:], b2_hi, b2_sign[:], b2_rows, ALU.mult, ALU.add).then_inc(setup_dve, 1)
            dve.wait_ge(small_in, 16 * 10)
            dve.wait_ge(setup_mm, 1)
            V.tensor_copy(rt_sb[:, 0:KC * E], bank[2][:, 0:KC * E]).then_inc(setup_dve, 1)

            def mean_var(L):
                ch.mark(tt(col["ta"], st(1), st(4), ALU.add))
                ch.mark(tt(col["tb"], st(1), st(4), ALU.subtract))
                ch.mark(tt(col["tc"], st(2), st(5), ALU.add))
                ch.wait()
                ch.mark(ts(col["mean"], col["ta"], 0.5, None, ALU.mult))
                ch.mark(stt(col["td"], col["tb"], 0.25, col["tb"], ALU.mult, ALU.mult))
                ch.wait()
                stt(col["var"], col["tc"], 1.0 / D, col["td"], ALU.mult, ALU.add).then_inc(var_ready[L], 1)

            def rstd_of(L, n, r, m):
                dve.wait_ge(sd_ready[L], at(n))
                ch.mark(V.reciprocal(col[r], col["sd"]))
                ch.wait()
                ch.mark(stt(col[m], col["mean"], -1.0, col[r], ALU.mult, ALU.mult))
                ch.wait()

            def soft(L, g):
                loop_wait(dve, E_ev[L], at(g + 1))
                loop_wait(dve, neg_ready[L], at(g + 1))
                if L == 1:
                    ch.mark(stt(scores, scores, LEAK, scores, ALU.mult, ALU.max))
                    ch.wait()
                ch.mark(tt(scores, scores, neg, ALU.add))
                ch.wait()
                s3 = scores.rearrange("p (t j) -> p t j", t=GT)
                ch.mark(V.tensor_reduce(rinv[:, GT:2 * GT], s3, AX.X, ALU.max))
                ch.wait()
                tt(s3, s3, bc(rinv[:, GT:2 * GT], NODES), ALU.subtract).then_inc(sm_ready[L], 1)

            def tokens_of(L, g):
                loop_wait(dve, G_mm[L], at(4 * g))
                for j in range(GT):
                    ins = ts(xn[:, j * D:(j + 1) * D], xs(g * GT + j), one("rstd", g * GT + j), one("nmr", g * GT + j), ALU.mult, ALU.add)
                    if j == GT - 1:
                        ins.then_inc(xn_ready[L], 1)
                loop_wait(dve, exp_done[L], at(g + 1))
                ch.mark(V.tensor_reduce(rinv[:, GT:2 * GT], probs.rearrange("p (t j) -> p t j", t=GT), AX.X, ALU.add))
                ch.wait()
                V.reciprocal(rinv[:, 0:GT], rinv[:, GT:2 * GT]).then_inc(rinv_ready[L], 1)

            def attend(L, g, more):
                if more:
                    soft(L, g + 1)
                for j in range(GT + 1):
                    if j < GT:
                        b = (j % 4) * D
                        loop_wait(dve, ER_done[L], at(8 * g + j + 1))
                        ch.mark(stt(er_e[:, b:b + D], er_e[:, b:b + D], 1.0, er_r[:, b:b + D], ALU.min, ALU.add))
                        ch.wait()
                        t = g * GT + j
                        stt(xs(t), er_e[:, b:b + D], -1.0, xs(t), ALU.add, ALU.add).then_inc(post[L], 1)
                        loop_wait(dve, post[L], at(8 * g + j + 1))
                        ch.mark(V.bn_stats(cut(stats, t * 6, 6), xs(t)))
                if more:
                    tokens_of(L, g + 1)

            PER_ATTEND = 2 + 2 * GT + 1
            for L in range(2):
                F = HID[L]
                FC = F // P
                for k in range(4):
                    ch.mark(V.tensor_copy(abc[:, k * P:(k + 1) * P], a_cols[:, L * 4 + k:L * 4 + k + 1].to_broadcast([P, P])))
                dve.wait_ge(setup_mm, 2 + 2 * L)
                V.tensor_copy(wgT[:], bank[0][:]).then_inc(setup_dve, 1)
                dve.wait_ge(setup_mm, 3 + 2 * L)
                ch.wait()
                V.tensor_copy(u_bc[:], bank[1][:]).then_inc(setup_dve, 1)
                dve.wait_ge(setup_dve, 4 + 2 * L)
                ch.mark(V.tensor_reduce(u_sum[:], u_bc[:].rearrange("p (j d) -> p j d", j=2), AX.X, ALU.add))

                if L == 0:
                    with dve.Fori(0, TILES // 16) as i:
                        ch.enter(i, 3 * 16)
                        for c in range(4):
                            loop_wait(dve, x_loaded[c], i * 16 + 16)
                            for v in range(4):
                                t = i * 16 + 4 * c + v
                                ch.mark(V.bn_stats(cut(stats, t * 6, 6), xs(t)))
                                dots(ch, t, v % 2)
                    ch.leave(TILES // 16)
                else:
                    combine(dve, ch, 0, True)
                ch.wait()
                ch.mark(V.memset(probs, 0.0))
                mean_var(L)
                rstd_of(L, 1, "rstd", "nmr")
                for j in range(2):
                    ch.mark(tt(col["ta"], col[f"dot{j + 1}"], col["rstd"], ALU.mult))
                    ch.wait()
                    ins = stt(col[f"s{j + 1}"], col["nmr"], u_sum[:, j:j + 1], col["ta"], ALU.mult, ALU.add)
                    if j == 0:
                        ch.mark(ins)
                        ch.wait()
                    else:
                        ins.then_inc(s_ready[L], 1)

                soft(L, 0)
                tokens_of(L, 0)
                with dve.Fori(0, GROUPS - 1) as g:
                    ch.enter(g, PER_ATTEND + L)
                    attend(L, g, True)
                ch.leave(GROUPS - 1)
                attend(L, GROUPS - 1, False)

                ch.wait()
                mean_var(L)
                rstd_of(L, 2, "rs2", "nm2")
                with dve.Fori(0, TILES // 8) as i:
                    for v in range(8 + 2):
                        t = i * 8 + v
                        if v < 8:
                            b = (v % 4) * D
                            loop_wait(dve, yT_mm[L], at(i * 4 + v // 2 - 1))
                            if v >= 4:
                                loop_wait(dve, yl_ready[L], at(t - 3))
                            if L == 0:
                                loop_wait(dve, x_plus_y[L], at(t - 3))
                            ts(y32[:, b:b + D], xs(t), one("rs2", t), one("nm2", t), ALU.mult, ALU.add).then_inc(y_ready[L], 1)
                        if 1 <= v < 9:
                            w = v - 1
                            if w % 4 == 0:
                                loop_wait(dve, y_stored[w // 4][L], 16 + i * 16)
                            loop_wait(dve, y_ready[L], at(t))
                            V.tensor_copy(y16[:, w * 512:w * 512 + D], y32[:, (w % 4) * D:(w % 4 + 1) * D]).then_inc(hi_ready[L], 1)
                        if 2 <= v:
                            w = v - 2
                            loop_wait(dve, hi_ready[L], at(t - 1))
                            tt(y16[:, w * 512 + D:(w + 1) * 512], y32[:, (w % 4) * D:(w % 4 + 1) * D],
                               y16[:, w * 512:w * 512 + D], ALU.subtract).then_inc(yl_ready[L], 1)

                dve.wait_ge(logit_mm[L], at(TILES // 2))
                dve.wait_ge(yl_ready[L], at(TILES))
                dve.wait_ge(yT_ev[L], at(TILES // 2))
                if L == 0:
                    dve.wait_ge(x_plus_y[L], at(TILES))
                for h in range(2):
                    dve.wait_ge(y_stored[h][L], 16 + 16 * (TILES // 8))
                te = lambda a: a.rearrange("p (t e) -> p t e", e=E)
                et = lambda a: a.rearrange("p (e t) -> p e t", e=E)
                if L == 0:
                    ch.mark(V.tensor_copy(lg, bank[7][:]))
                else:
                    ch.mark(tt(te(lg), te(bank[7][:]), rows(gb_bc[:, 0:E], TILES), ALU.add))
                    ch.wait()
                    ch.mark(tt(te(lg), te(lg), rows(gb_bc[:, E:2 * E], TILES), ALU.add))
                ch.wait()
                for src, mx, M in ((lg, "m1", M1), (lg2, "m2", M2)):
                    ch.mark(V.tensor_reduce(col[mx], te(src), AX.X, ALU.max))
                    ch.wait()
                    ch.mark(tt(te(eqm), te(src), bc(col[mx], E), ALU.is_equal))
                    ch.wait()
                    ch.mark(tt(te(sc), te(eqm), rows(rank8[:], TILES), ALU.mult))
                    ch.wait()
                    ch.mark(V.tensor_reduce(col["rk"], te(sc), AX.X, ALU.max))
                    ch.wait()
                    ch.mark(tt(te(M), te(sc), bc(col["rk"], E), ALU.is_equal))
                    ch.wait()
                    if M is M1:
                        ch.mark(stt(lg2, M1, -3.0e38, lg, ALU.mult, ALU.add))
                        ch.wait()
                tt(col["tb"], col["m2"], col["m1"], ALU.subtract).then_inc(gap_ready[L], 1)
                tt(msum[:, 0:512], M1, M2, ALU.add).then_inc(msum_ready[L], 1)
                ch.mark(V.memset(onesd, 1.0))
                dve.wait_ge(rank_mm[L], at(1))
                ch.mark(V.tensor_copy(et(big_a), bank[1][:].rearrange("p (t e) -> p e t", e=E)))
                ch.wait()
                ch.mark(V.tensor_tensor_scan(big_b, onesd, big_a, 0.0, ALU.mult, ALU.add))
                ch.wait()
                ends, cnt, nt, tiles_to, base, adj_e, zero8 = (ex[:, 9 * k:9 * k + 9] for k in range(7))
                ch.mark(V.memset(ex[:], 0.0))
                ch.wait()
                ch.mark(V.tensor_copy(ends[:, 1:9].rearrange("p (e one) -> p e one", one=1), et(big_b)[:, :, TILES - 1:TILES]))
                ch.wait()
                ch.mark(tt(cnt[:, 0:E], ends[:, 1:9], ends[:, 0:8], ALU.subtract))
                ch.wait()
                ch.mark(ts(ex_i[:, 0:E], cnt[:, 0:E], float(SLOT - 1), None, ALU.add))
                ch.wait()
                ch.mark(ts(ex_i[:, E:2 * E], ex_i[:, 0:E], SLOT.bit_length() - 1, None, ALU.arith_shift_right))
                ch.wait()
                ch.mark(V.tensor_copy(nt[:, 0:E], ex_i[:, E:2 * E]))
                ch.wait()
                ch.mark(V.tensor_tensor_scan(tiles_to[:, 0:E], onesd[:, 0:E], nt[:, 0:E], 0.0, ALU.mult, ALU.add))
                ch.wait()
                ch.mark(tt(base[:, 0:E], tiles_to[:, 0:E], nt[:, 0:E], ALU.subtract))
                ch.wait()
                ch.mark(stt(adj_e[:, 0:E], base[:, 0:E], float(SLOT), ends[:, 0:8], ALU.mult, ALU.subtract))
                ch.mark(tt(big_b, big_b, big_a, ALU.subtract))
                ch.wait()
                ch.mark(tt(et(big_b), et(big_b), bc(adj_e[:, 0:E], TILES), ALU.add))
                ch.wait()
                ch.mark(tt(pf.rearrange("p (t e) -> p e t", e=E), et(big_b), bank[0][:].rearrange("p (t e) -> p e t", e=E), ALU.add))
                ch.wait()
                for k, M in enumerate((M1, M2)):
                    ch.mark(tt(big_a, M, pf, ALU.mult))
                    ch.wait()
                    ch.mark(V.tensor_reduce(col["rk"], te(big_a), AX.X, ALU.add))
                    ch.wait()
                    ch.mark(V.tensor_copy(pos_i[k][:], col["rk"]))
                    ch.wait()
                    ch.mark(ts(tmp_i[:], pos_i[k][:], P - 1, None, ALU.bitwise_and))
                    ch.wait()
                    ch.mark(V.tensor_copy(col[f"lo{k}"], tmp_i[:]))
                    ch.wait()
                    ch.mark(ts(tmp_i[:], pos_i[k][:], 7, None, ALU.arith_shift_right))
                    ch.wait()
                    ch.mark(V.tensor_copy(col[f"hi{k}"], tmp_i[:]))
                    ch.wait()
                ch.mark(V.memset(inv_a[:, 0:P], 0.0))
                ch.wait()
                V.memset(inv_b[:, 0:2 * STILES], 0.0).then_inc(ab_ready[L], 1)
                dve.wait_ge(inv_mm[L], at(1))
                with dve.Fori(0, TILES // 4) as i:
                    for v in range(4):
                        for k in range(2):
                            b, t = 2 * v + k, 4 * i + v
                            if b % 4 == 0:
                                loop_wait(dve, inv_mm[L], at(8 * i + b - 3))
                            o = 2 * b * STILES
                            ts(inv_a[:, b * P:(b + 1) * P], iota_p[:], one(f"lo{k}", t), None, ALU.is_equal)
                            ts(inv_b[:, o:o + STILES], iota_s[:], one(f"hi{k}", t), cut(row_id, TILES * k + t, 1), ALU.is_equal, ALU.mult)
                            ts(inv_b[:, o + STILES:o + 2 * STILES], iota_s[:], one(f"hi{k}", t), part_id[:],
                               ALU.is_equal, ALU.mult).then_inc(ab_ready[L], 1)
                dve.wait_ge(inv_mm[L], at(2 * TILES + 1))
                ch.mark(V.memset(inv_a[:, 0:P], 0.0))
                ch.wait()
                V.memset(inv_b[:, 0:2 * STILES], 0.0).then_inc(ab_ready[L], 1)
                ct = cmp_t[0:1, :].rearrange("p (s e) -> p s e", e=E)
                ch.mark(tt(ct, tiles_to[0:1, 0:E].rearrange("p (one e) -> p one e", one=1).to_broadcast([1, SLOTS, E]),
                           iota_sf[:].rearrange("p (s one) -> p s one", one=1).to_broadcast([1, SLOTS, E]), ALU.is_le))
                ch.wait()
                ch.mark(V.tensor_reduce(big_a[0:1, 0:SLOTS], ct, AX.X, ALU.add))
                ch.wait()
                ch.mark(ts(slot_expert[:, 0:SLOTS], big_a[0:1, 0:SLOTS], float(E - 1), None, ALU.min))
                ch.mark(ts(slot_block[:, 0:SLOTS], big_a[0:1, 0:SLOTS], float(E - 1), float(8 * F + D), ALU.min, ALU.mult))
                dve.wait_ge(e2_ready[L], at(1))
                ch.mark(ts(col["tc"], col["ta"], 1.0, None, ALU.add))
                ch.wait()
                ch.mark(V.reciprocal(col["w1"], col["tc"]))
                ch.wait()
                ch.mark(tt(col["w2"], col["ta"], col["w1"], ALU.mult))
                ch.wait()
                dve.wait_ge(inv_mm[L], at(2 * TILES + 2))
                ch.mark(V.tensor_copy(inv_w, bank[2][:, STILES:2 * STILES]))
                ch.wait()
                ch.mark(stt(inv_v, bank[2][:, 0:STILES], float(P), inv_w, ALU.mult, ALU.add))
                ch.wait()
                ch.mark(ts(inv_i, inv_v, -1.0, None, ALU.add))
                ch.mark(stt(inv_x, inv_v, 0.0, dump_id[:], ALU.is_equal, ALU.mult))
                ch.wait()
                ch.mark(stt(scatter_row[:], inv_v, -1.0, inv_x, ALU.add, ALU.add))
                ch.wait()
                ts(gather_row[:].bitcast(I32), inv_i, TOKENS - 1, None, ALU.bitwise_and).then_inc(slots_ready[L], 1)

                def copy_T(s, u):
                    loop_wait(dve, T_mm[L], at(s + 1))
                    loop_wait(dve, h_mm[L], at(s - 1))
                    V.tensor_copy(tT[:, (u % 2) * 4 * SLOT:(u % 2 + 1) * 4 * SLOT], bank[u % 2][:].bitcast(F16)).then_inc(T_ev[L], 1)

                def cut_hidden(s, u):
                    loop_wait(dve, h_act[L], at(s + 1))
                    loop_wait(dve, o_mm[L], at(s - 1))
                    hb = (u % 2) * 4 * SLOT
                    ch.mark(V.tensor_copy(hid_hi[:, hb:hb + FC * SLOT], hid[:, hb:hb + FC * SLOT]))
                    ch.wait()
                    tt(hid_lo[:, hb:hb + FC * SLOT], hid[:, hb:hb + FC * SLOT], hid_hi[:, hb:hb + FC * SLOT], ALU.subtract).then_inc(h_split[L], 1)

                def experts(i, more):
                    for u in range(SU):
                        s = i * SU + u
                        if more or u + 1 < SU:
                            cut_hidden(s + 1, u + 1)
                        if more or u + 3 < SU:
                            copy_T(s + 3, u + 3)

                copy_T(0, 0)
                copy_T(1, 1)
                copy_T(2, 2)
                cut_hidden(0, 0)
                with dve.Fori(0, TURNS - 1) as i:
                    ch.enter(i, SU)
                    experts(i, True)
                ch.leave(TURNS - 1)
                experts(TURNS - 1, False)
            combine(dve, ch, 1, False)


_INS = ["x", "adj", "L0_gnn_W", "L0_gnn_a", "L0_ffn_router_w", "L0_ffn_w1", "L0_ffn_b1", "L0_ffn_w2", "L0_ffn_b2",
        "L1_gnn_W", "L1_gnn_a", "L1_ffn_Wg", "L1_ffn_bg", "L1_ffn_bias", "L1_ffn_W1", "L1_ffn_b1", "L1_ffn_W2", "L1_ffn_b2"]


def kernel(**inputs):
    import numpy as _np
    import concourse.bacc as _bacc
    from concourse import mybir as _mybir
    from concourse.bass_utils import run_bass_kernel_spmd as _run

    nc = _bacc.Bacc("TRN2", target_bir_lowering=False, num_devices=1)
    arrays, t = {}, {}
    for name in _INS:
        a = _np.ascontiguousarray(inputs[name])
        arrays[f"in_{name}"] = a
        t[name] = nc.dram_tensor(f"in_{name}", a.shape, _mybir.dt.from_np(a.dtype), kind="ExternalInput").ap()
    out = nc.dram_tensor("out_0", (GRAPHS, NODES, D), F32, kind="ExternalOutput").ap()
    build(nc, t["x"], t["adj"], (t["L0_gnn_W"], t["L1_gnn_W"]), (t["L0_gnn_a"], t["L1_gnn_a"]),
          (t["L0_ffn_router_w"], t["L1_ffn_Wg"]), t["L1_ffn_bg"], t["L1_ffn_bias"],
          (t["L0_ffn_w1"], t["L1_ffn_W1"]), (t["L0_ffn_b1"], t["L1_ffn_b1"]),
          (t["L0_ffn_w2"], t["L1_ffn_W2"]), (t["L0_ffn_b2"], t["L1_ffn_b2"]), out)
    r = _run(nc, [arrays], core_ids=[0])
    return r.results[0]["out_0"]
```

```python
import concourse.bass as bass
from concourse import mybir
from contextlib import ExitStack

F32 = mybir.dt.float32
F16 = mybir.dt.float16
I32 = mybir.dt.int32
U32 = mybir.dt.uint32
ALU = mybir.AluOpType
ACT = mybir.ActivationFunctionType
AX = mybir.AxisListType

P = 128
GRAPHS = 128
NODES = 64
D = 256
KC = D // P
TOKENS = GRAPHS * NODES
TILES = TOKENS // P
GT = 8
GROUPS = TILES // GT
E = 8
TOPK = 2
SLOT = 256
ST = SLOT // P
SLOTS = TOKENS * TOPK // SLOT + E
STILES = SLOTS * ST
SU = 4
SV = SU * ST
AHEAD_G = 12
HID = (256, 512)
NEG_BIG = -9000000000000000.0
EPS = 1e-5
LEAK = 0.2
WSCALE = 64.0
AHEAD = 16


def at(n):
    return n + AHEAD


def build(nc, x_in, adj, W_gnn, a_gnn, router, gate_b, gate_bias, w1, b1, w2, b2, out):
    ctx = ExitStack()
    with ctx:
        def sb(name, shape, dt=F32):
            return ctx.enter_context(nc.sbuf_tensor(name, shape, dt))

        def sem(name):
            return ctx.enter_context(nc.semaphore(name))

        def sem2(name):
            return [ctx.enter_context(nc.semaphore(f"{name}_{L}")) for L in range(2)]

        table = [nc.dram_tensor(f"split_tokens_{L}", (TOKENS, 2 * D), F16, kind="Internal").ap() for L in range(2)]
        ydram = [nc.dram_tensor(f"expert_outputs_{L}", (TOPK * TOKENS + STILES * P, D), F32, kind="Internal").ap() for L in range(2)]

        X = sb("X", [P, TILES * D])
        WREG = sb("WREG", [P, E * 8 * HID[1]], F16)
        ident = sb("ident", [P, P])
        ident16 = sb("ident16", [P, P], F16)
        before16 = sb("before16", [P, P], F16)
        ones16 = sb("ones16", [P, P], F16)
        ones32 = sb("ones32", [P, P])
        same_graph = sb("same_graph", [P, P])
        stacked_id = sb("stacked_id", [P, NODES])
        iota_p = sb("iota_p", [P, P])
        iota_s = sb("iota_s", [P, STILES])
        row_id = sb("row_id", [P, TOPK * TILES])
        dump_id = sb("dump_id", [P, STILES])
        rank8 = sb("rank8", [P, E])
        eps_col = sb("eps_col", [P, 1])
        wg_sb = sb("wg_sb", [P, 2 * KC * D])
        a_cols = sb("a_cols", [P, 2 * 4])
        wgT = sb("wgT", [P, KC * D])
        rt_sb = sb("rt_sb", [P, 2 * KC * E])
        rt_rows = sb("rt_rows", [E, D])
        rt16 = sb("rt16", [P, 2 * KC * 2 * E], F16)
        u_cols = sb("u_cols", [P, KC * 2])
        u_sum = sb("u_sum", [P, 2])
        gb_bc = sb("gb_bc", [P, 2 * E])
        b1T = sb("b1T", [P, E * (HID[0] + HID[1]) // P])
        b2_bc = sb("b2_bc", [P, E * D])
        stats = sb("stats", [P, TILES * 6])
        cols = sb("cols", [P, 24 * TILES])
        names = ["mean", "rstd", "nmr", "s1", "s2", "ta", "tb", "tc", "w1", "w2",
                 "m1", "m2", "rk", "lo0", "hi0", "lo1", "hi1", "rs2", "nm2", "var", "sd", "td", "dots", "dots_end"]
        dots = cols[:, 22 * TILES:24 * TILES]
        col = {n: cols[:, k * TILES:(k + 1) * TILES] for k, n in enumerate(names)}

        pos_i = [sb(f"pos_i{k}", [P, TILES], I32) for k in range(TOPK)]
        tmp_i = sb("tmp_i", [P, TILES], I32)
        gather_row = sb("gather_row", [P, STILES], U32)
        scatter_row = sb("scatter_row", [P, STILES], U32)
        slot_expert = sb("slot_expert", [1, SLOTS], I32)
        slot_block = sb("slot_block", [1, SLOTS], I32)
        ex = sb("ex", [P, 6 * 9])
        ex_i = sb("ex_i", [P, 2 * E], I32)
        gather_now = sb("gather_now", [P, SV], U32)
        scatter_now = sb("scatter_now", [P, SV], U32)
        soft_cols = sb("soft_cols", [P, 3 * GT])
        rinv, row_max, row_sum = (soft_cols[:, k * GT:(k + 1) * GT] for k in range(3))

        arena = sb("arena", [P, 9728])
        used = [0]

        def carve(n, start=None):
            if start is not None:
                used[0] = start
            a = arena[:, used[0]:used[0] + n]
            used[0] += n
            assert used[0] <= 9728
            return a

        neg = carve(512, 8704)
        adj_sb = carve(512).bitcast(I32)
        diag = carve(512, 0)
        scores = carve(512)
        probs = carve(GT * P)
        probsT = carve(GT * P)
        xn = carve(GT * D)
        gT = carve(2 * 2 * D)
        er_e = carve(4 * D)
        er_r = carve(4 * D)
        stage_w = sb("stage_w", [P, 2048])
        comb = carve(4 * 8 * D, 0)
        xT = carve(2 * 2 * D, 2 * 8 * D)
        x_now = carve(8 * D)
        u_rows = carve(2 * D, 0)
        junk = carve(8 * D)
        y32 = carve(8 * D, 0)
        y16 = carve(16 * D).bitcast(F16)
        yT = carve(2 * 2 * D).bitcast(F16)
        lg, eqm, sc, M1, M2, lg2, pf, big_a, big_b, onesd = (carve(512, 0 if k == 0 else None) for k in range(10))
        cmp_t = carve(SLOTS * E)
        msum = carve(256).bitcast(F16)
        inv_a = carve(8 * P)
        inv_d = carve(8 * P)
        inv_b = carve(8 * STILES)
        inv_v, inv_x = (carve(STILES) for _ in range(2))
        inv_i = carve(STILES).bitcast(I32)
        gat = carve(SV * D, 0).bitcast(F16)
        tT = carve(2 * 2 * SLOT).bitcast(F16)
        hid = carve(2 * 4 * SLOT)
        hid_hi = carve(4 * SLOT).bitcast(F16)
        hid_lo = carve(4 * SLOT).bitcast(F16)
        o_sb = carve(SV * D)

        bank = [ctx.enter_context(nc.psum_tensor(f"bank{k}", [P, 512], F32)) for k in range(8)]

        go = sem("go")
        pool_tick = sem("pool_tick")
        const_pool = sem("const_pool")
        const_ready = sem("const_ready")
        small_in = sem("small_in")
        b2_in = sem("b2_in")
        setup_dve = sem("setup_dve")
        setup_mm = sem("setup_mm")
        u_mm = sem("u_mm")
        x_loaded = [sem(f"x_loaded_{k}") for k in range(4)]
        adj_loaded, out_stored = sem2("adj_loaded"), sem("out_stored")
        weights_loaded = [sem2(f"weights_loaded_{k}") for k in range(2)]
        y_stored = [sem2(f"y_stored_{k}") for k in range(4)]
        gathered = [sem(f"gathered_{k}") for k in range(SU)]
        scattered = [sem(f"scattered_{k}") for k in range(SV)]
        c_loaded = [sem(f"c_loaded_{k}") for k in range(4)]
        own = sem("dve_own")
        diff_ready, neg_ready, diag_ready, scaled, split_done, x_plus_y, idx_ready, sidx_ready = by_pool = [sem2(n) for n in (
            "diff_ready", "neg_ready", "diag_ready", "scaled", "split_done", "x_plus_y", "idx_ready", "sidx_ready")]
        xT_mm, dot_mm, E_mm, PT_mm, G_mm, H_mm, yT_mm, logit_mm, rank_mm, inv_mm, T_mm, h_mm, o_mm = by_pe = [sem2(n) for n in (
            "xT_mm", "dot_mm", "E_mm", "PT_mm", "G_mm", "H_mm", "yT_mm", "logit_mm", "rank_mm", "inv_mm", "T_mm", "h_mm", "o_mm")]
        (E_ev, exp_done, PT_ev, G_ev, xn_half, ER_done, x_copied, xT_ev, y_ready, sd_ready, high_ready, abs_ready,
         onehot_ready, e2_ready, h_act) = by_act = [sem2(n) for n in (
            "E_ev", "exp_done", "PT_ev", "G_ev", "xn_half", "ER_done", "x_copied", "xT_ev", "y_ready", "sd_ready",
            "high_ready", "abs_ready", "onehot_ready", "e2_ready", "h_act")]
        (combined, var_ready, s_ready, sm_ready, xn_ready, post, rinv_ready, rs2_ready, hi_ready, yT_ev, yl_ready, gap_ready,
         msum_ready, ab_ready, slots_ready, T_ev, h_split, o_ev) = by_dve = [sem2(n) for n in (
            "combined", "var_ready", "s_ready", "sm_ready", "xn_ready", "post", "rinv_ready", "rs2_ready", "hi_ready",
            "yT_ev", "yl_ready", "gap_ready", "msum_ready", "ab_ready", "slots_ready", "T_ev", "h_split", "o_ev")]

        def credit(eng, sems):
            for pair in sems:
                for s in pair:
                    eng.sem_inc(s, AHEAD)

        def loop_wait(eng, s, value):
            eng.wait_ge(s, value)
            eng.wait_ge(go, 1)

        def used_before(L, i):
            return L > 0 or not isinstance(i, int) or i > 0

        class Chain:

            def __init__(self, eng, s):
                self.eng, self.s, self.n, self.base = eng, s, 0, 0

            def mark(self, ins):
                ins.then_inc(self.s, 1)
                self.n += 1
                return self.n

            def wait(self, n=None):
                loop_wait(self.eng, self.s, self.base + (self.n if n is None else n))

            def enter(self, i, per_turn):
                self.base, self.start, self.per = i * per_turn, self.n, per_turn

            def leave(self, turns):
                assert self.n - self.start == self.per, (self.n - self.start, self.per)
                self.base, self.n = 0, self.start + self.per * turns

        block = ctx.enter_context(nc.Block())

        xt_dram = x_in.rearrange("(t two) n d -> (two n) t d", two=2)
        out_dram = out.rearrange("(t two) n d -> (two n) t d", two=2)
        adj_dram = adj.rearrange("(t two) i j -> (two i) t j", two=2)
        TURNS = SLOTS // SU
        X_TURNS = (TILES // 16, TILES // 8)

        def cut(a, start, n):
            return a[:, start:start + n] if isinstance(start, int) else a[:, bass.ds(start, n)]

        def cut3(a, start, n):
            return a[:, start:start + n, :] if isinstance(start, int) else a[:, bass.ds(start, n), :]

        def xs(t, n=1):
            return cut(X, t * D, n * D)

        def one(name, t, n=1):
            return cut(cols, names.index(name) * TILES + t, n)

        def bc(a, n):
            return a.rearrange("p (m one) -> p m one", one=1).to_broadcast([P, a.shape[1], n])

        def rows(a, n):
            return a.rearrange("p (one m) -> p one m", one=1).to_broadcast([P, n, a.shape[1]])

        def w1_at(L, e, hl, kc, fc):
            return cut(WREG, e + ((hl * KC + kc) * HID[L] + fc * P), P)

        def w2_at(L, e, hl, fc):
            return cut(WREG, e + (4 * HID[L] + (hl * (HID[L] // P) + fc) * D), D)

        def weight_parts(L, e, k):
            n = 2 * HID[L]
            return (stage_w[:, n * k:n * (k + 1)],) + tuple(cut(WREG, e * (4 * n) + (2 * k + h) * n, n) for h in range(2))

        slot_regs = {}

        def of_slots(eng, table, i, n, per):
            if (eng, table.name) not in slot_regs:
                slot_regs[eng, table.name] = [eng.alloc_register(f"{table.name}_{k}") for k in range(SU + 2)]
            eng.reg_load(slot_regs[eng, table.name][:n], cut(table, i * SU, n))
            return [eng.snap(r, min_val=0, max_val=(E - 1) * per) for r in slot_regs[eng, table.name][:n]]

        def load_outputs(sp, L):
            for u in range(SV):
                sp.wait_ge(scattered[u], 16 * TURNS * (L + 1))
            n = 2 + 2 * L

            def load(i, h):
                for k in range(TOPK):
                    sp.dma_start(comb[:, (8 * h + 4 * k) * D:(8 * h + 4 * k + 4) * D].rearrange("p (t d) -> p t d", d=D),
                                 cut3(ydram[L][0:TOPK * TOKENS, :].rearrange("(t p) d -> p t d", p=P), i * (4 * n) + (4 * h + TILES * k), 4)
                                 ).then_inc(c_loaded[h], 16)

            def store(t):
                sp.dma_start(cut3(out_dram, t, 4), xs(t, 4).rearrange("p (t d) -> p t d", d=D)).then_inc(out_stored, 16)

            for h in range(n):
                load(0, h)
            with sp.Fori(1, TILES // (4 * n)) as i:
                for h in range(n):
                    t = (i - 1) * (4 * n) + 4 * h
                    sp.wait_ge(combined[L], at(t + 4))
                    load(i, h)
                    if L:
                        store(t)
            if L:
                for t in range(TILES - 4 * n, TILES, 4):
                    sp.wait_ge(combined[L], at(t + 4))
                    store(t)

        def combine(dve, ch, L, stats_too):
            V = nc.vector
            marks = {}
            n = 2 + 2 * L

            def add(k, i, h):
                for v in range(4):
                    t = i * (4 * n) + 4 * h + v
                    o = (8 * h + 4 * k + v) * D
                    ins = V.scalar_tensor_tensor(xs(t), comb[:, o:o + D], one(f"w{k + 1}", t), xs(t), ALU.mult, ALU.add)
                    if k == 1:
                        ins.then_inc(combined[L], 1)
                if k == 0:
                    marks[h] = ch.mark(ins)

            with dve.Fori(0, TILES // (4 * n)) as i:
                ch.enter(i, n + (4 * n if stats_too else 0))
                for h in range(n + 1):
                    if h < n:
                        before = 32 * (TILES // 8) if L and h < 2 else 0
                        loop_wait(dve, c_loaded[h], before + i * 32 + 32)
                        add(0, i, h)
                    if stats_too and h:
                        loop_wait(dve, combined[L], at(i * (4 * n) + 4 * h))
                        for v in range(4):
                            t = i * (4 * n) + 4 * (h - 1) + v
                            ch.mark(V.bn_stats(cut(stats, t * 6, 6), xs(t)))
                    if h < n:
                        ch.wait(marks[h])
                        add(1, i, h)
            ch.leave(TILES // (4 * n))

        @block.sync
        def _(sp):
            sp.sem_inc(go, 1)
            for L in range(2):
                for h in range(4):
                    sp.sem_inc(y_stored[h][L], 16)
            for L in range(2):
                sp.dma_start(wg_sb[:, L * KC * D:(L + 1) * KC * D].rearrange("p (k n) -> p k n", k=KC),
                             W_gnn[L].rearrange("(k p) n -> p k n", p=P)).then_inc(small_in, 16)
                with nc.allow_non_contiguous_dma(reason="vectors onto partitions"):
                    sp.dma_start(a_cols[:, L * 4:(L + 1) * 4],
                                 a_gnn[L].rearrange("(k p) one -> p (k one)", p=P)).then_inc(small_in, 16)
                    base = L * E * HID[0] // P
                    sp.dma_start(b1T[:, base:base + E * HID[L] // P].rearrange("p (e c) -> p e c", e=E),
                                 b1[L].rearrange("e (c p) -> p e c", p=P)).then_inc(small_in, 16)
            sp.dma_start(rt_rows[:], router[0]).then_inc(small_in, 16)
            sp.dma_start(rt_sb[:, KC * E:2 * KC * E].rearrange("p (k n) -> p k n", k=KC),
                         router[1].rearrange("(k p) n -> p k n", p=P)).then_inc(small_in, 16)
            for k, v in enumerate((gate_b, gate_bias)):
                sp.dma_start(gb_bc[:, k * E:(k + 1) * E],
                             v.rearrange("(one e) -> one e", one=1).to_broadcast([P, E])).then_inc(small_in, 16)
            for c in range(TILES // 4):
                if c >= 4:
                    sp.wait_ge(x_loaded[c % 4], 16 * (c // 4))
                sp.dma_start(xs(4 * c, 4).rearrange("p (t d) -> p t d", d=D),
                             xt_dram[:, 4 * c:4 * c + 4, :]).then_inc(x_loaded[c % 4], 16)

            for L in range(2):
                F = HID[L]
                sp.dma_start(b2_bc[:], b2[L].rearrange("(one e) d -> one (e d)", one=1).to_broadcast([P, E * D])).then_inc(b2_in, 16)
                def load_weights(e, k):
                    n = F // P if k else KC
                    src = w2[L].rearrange("e (k p) n -> p (e k) n", p=P) if k else w1[L].rearrange("e (k p) f -> p (e k) f", p=P)
                    sp.wait_ge(split_done[L], at(2 * e + k - 1))
                    sp.dma_start(stage_w[:, 2 * F * k:2 * F * (k + 1)].rearrange("p (k f) -> p k f", k=n),
                                 cut3(src, e * n, n)).then_inc(weights_loaded[k][L], 16)

                with sp.Fori(0, GROUPS // 2) as g:
                    for k in range(2):
                        sp.wait_ge(neg_ready[L], at(2 * g + k))
                        sp.dma_start(adj_sb.rearrange("p (t j) -> p t j", t=GT),
                                     adj_dram[:, bass.ds(g * (2 * GT) + k * GT, GT), :]).then_inc(adj_loaded[L], 16)
                        load_weights(g, k)
                for k in range(2):
                    load_weights(E // 2, k)
                with sp.Fori(0, TILES // 16) as i:
                    for h in range(4):
                        sp.wait_ge(yl_ready[L], at(i * 8 + 2 * h + 2))
                        sp.dma_start(table[L].rearrange("(t p) c -> p t c", p=P)[:, bass.ds(i * 16 + 4 * h, 4), :],
                                     y16[:, 4 * h * 512:(4 * h + 4) * 512].rearrange("p (t c) -> p t c", t=4)).then_inc(y_stored[h][L], 16)
                with sp.Fori(E // 2 + 1, E) as e:
                    for k in range(2):
                        load_weights(e, k)
                load_outputs(sp, L)
            sp.wait_ge(out_stored, 16 * (TILES // 4))

        @block.gpsimd
        def _(pool):
            credit(pool, by_pool)
            n = 0

            def step(ins):
                nonlocal n
                n += 1
                ins.then_inc(const_pool, 1)
                pool.wait_ge(const_pool, n)

            for t_, v in ((ident, 0.0), (ident16, 0.0), (before16, 1.0), (same_graph, 0.0), (stacked_id, 0.0),
                          (ones16, 1.0), (ones32, 1.0), (eps_col, EPS)):
                step(nc.gpsimd.memset(t_[:], v))
            for t_ in (ident, ident16):
                step(nc.gpsimd.affine_select(out=t_[:], in_=t_[:], compare_op=ALU.not_equal, fill=1.0, base=0,
                                             pattern=[[-1, P]], channel_multiplier=1))
            step(nc.gpsimd.affine_select(out=before16[:], in_=before16[:], compare_op=ALU.is_gt, fill=0.0, base=0,
                                         pattern=[[1, P]], channel_multiplier=-1))
            step(nc.gpsimd.memset(same_graph[0:NODES, 0:NODES], 1.0))
            step(nc.gpsimd.memset(same_graph[NODES:P, NODES:P], 1.0))
            for b in (0, NODES):
                step(nc.gpsimd.affine_select(out=stacked_id[:], in_=stacked_id[:], compare_op=ALU.not_equal, fill=1.0,
                                             base=-b, pattern=[[-1, NODES]], channel_multiplier=1))
            for t_, pat, base, cm in ((iota_p[:], [[1, P]], 0, 0), (iota_s[:], [[1, STILES]], 0, 0),
                                      (row_id[:], [[P, TOPK * TILES]], 1, 1), (dump_id[:], [[P, STILES]], TOPK * TOKENS + 1, 1),
                                      (rank8[:], [[-1, E]], E, 0)):
                step(nc.gpsimd.iota(t_, pattern=pat, base=base, channel_multiplier=cm,
                                    allow_small_or_imprecise_dtypes=True))
            nc.gpsimd.memset(gather_now[:], 0).then_inc(const_ready, 1)

            for L in range(2):
                F = HID[L]
                def cut_weights(e, k):
                    stage, hi, lo = weight_parts(L, e, k)
                    pool.wait_ge(weights_loaded[k][L], e * 16 + 16)
                    pool.sem_inc(pool_tick)
                    nc.gpsimd.tensor_scalar(stage, stage, WSCALE, None, ALU.mult).then_inc(scaled[L], 1)
                    loop_wait(pool, scaled[L], at(e * 4 + 2 * k + 1))
                    nc.gpsimd.tensor_copy(hi, stage).then_inc(scaled[L], 1)
                    loop_wait(pool, scaled[L], at(e * 4 + 2 * k + 2))
                    nc.gpsimd.tensor_tensor(lo, stage, hi, ALU.subtract).then_inc(split_done[L], 1)

                with pool.Fori(0, GROUPS // 2) as i:
                    for k in range(2):
                        g = 2 * i + k
                        pool.wait_ge(sm_ready[L], at(g))
                        pool.wait_ge(adj_loaded[L], g * 16 + 16)
                        pool.sem_inc(pool_tick)
                        nc.gpsimd.tensor_scalar(neg, adj_sb, 0, NEG_BIG, ALU.is_le, ALU.mult).then_inc(neg_ready[L], 1)
                        pool.wait_ge(s_ready[L], at(1))
                        loop_wait(pool, E_mm[L], at(g))
                        nc.gpsimd.tensor_tensor(diag.rearrange("p (t j) -> p t j", t=GT), rows(stacked_id[:], GT),
                                                bc(one("s2", g * GT, GT), NODES), ALU.mult).then_inc(diag_ready[L], 1)
                        cut_weights(i, k)
                if L == 0:
                    with pool.Fori(0, TILES // 8) as i:
                        for q in range(4):
                            loop_wait(pool, y_ready[L], at(i * 4 + q + 1))
                            nc.gpsimd.tensor_tensor(xs(i * 8 + 2 * q, 2), xs(i * 8 + 2 * q, 2), y32[:, 2 * q * D:2 * (q + 1) * D],
                                                    ALU.add).then_inc(x_plus_y[L], 1)
                with pool.Fori(E // 2, E) as e:
                    for k in range(2):
                        stage, hi, lo = weight_parts(L, e, k)
                        loop_wait(pool, high_ready[L], at((e - E // 2) * 2 + k + 1))
                        nc.gpsimd.tensor_tensor(lo, stage, hi, ALU.subtract).then_inc(split_done[L], 1)
                pool.wait_ge(ab_ready[L], at(1))
                with pool.Fori(0, TILES // 4) as i:
                    for k in range(TOPK):
                        loop_wait(pool, onehot_ready[L], at(2 * i + k - 1))
                        nc.gpsimd.tensor_tensor(inv_d[:, 4 * k * P:4 * (k + 1) * P].rearrange("p (t m) -> p t m", t=4),
                                                rows(iota_p[:], 4), bc(one(f"lo{k}", 4 * i, 4), P),
                                                ALU.subtract).then_inc(diff_ready[L], 1)
                for h in range(4):
                    pool.wait_ge(y_stored[h][L], 16 + 16 * (TILES // 16))
                pool.wait_ge(slots_ready[L], at(1))

                def gather(i, u, t):
                    if u % 4 == 0:
                        loop_wait(pool, T_mm[L], at((i - 1) * SU + u // 2 + 2))
                        nc.gpsimd.tensor_copy(gather_now[:, u:u + 4], cut(gather_row, t, 4)).then_inc(idx_ready[L], 1)
                        pool.wait_ge(idx_ready[L], at(i * 2 + u // 4 + 1))
                        pool.sem_inc(pool_tick)
                    nc.gpsimd.indirect_dma_start(
                        out=gat[:, u * 512:(u + 1) * 512], out_offset=None, in_=table[L],
                        in_offset=bass.IndirectOffsetOnAxis(ap=gather_now[:, u:u + 1], axis=0)).then_inc(gathered[u // ST], 16)

                def scatter(i, u, t):
                    if u % 4 == 0:
                        for v in range(4):
                            if used_before(L, i):
                                loop_wait(pool, scattered[u + v], 16 * TURNS * L + 16 * i)
                        nc.gpsimd.tensor_copy(scatter_now[:, u:u + 4], cut(scatter_row, t, 4)).then_inc(sidx_ready[L], 1)
                        pool.wait_ge(sidx_ready[L], at(i * 2 + u // 4 + 1))
                    if u % ST == 0:
                        pool.wait_ge(o_ev[L], at(i * SU + u // ST + 1))
                        pool.sem_inc(pool_tick)
                    nc.gpsimd.indirect_dma_start(
                        out=ydram[L], out_offset=bass.IndirectOffsetOnAxis(ap=scatter_now[:, u:u + 1], axis=0),
                        in_=o_sb[:, u * D:(u + 1) * D], in_offset=None).then_inc(scattered[u], 16)

                def move(i, left):
                    for u in range(SV):
                        t = i * SV + u
                        if u + AHEAD_G < (left + 1) * SV:
                            gather(i + (u + AHEAD_G) // SV, (u + AHEAD_G) % SV, t + AHEAD_G)
                        scatter(i, u, t)

                for t in range(AHEAD_G):
                    gather(t // SV, t % SV, t)
                move(0, 2)
                with pool.Fori(1, TURNS - 2) as i:
                    move(i, 2)
                move(TURNS - 2, 1)
                move(TURNS - 1, 0)

        @block.tensor
        def _(pe):
            credit(pe, by_pe)
            mm = nc.tensor.matmul
            pe.wait_ge(const_ready, 1)
            pe.wait_ge(small_in, 16 * 10)
            for c in range(KC):
                last = nc.tensor.transpose(bank[2][:, c * E:(c + 1) * E], rt_rows[:, c * P:(c + 1) * P], ident[0:E, 0:E])
            last.then_inc(setup_mm, 1)

            def edge_vectors(L):
                for oc in range(KC):
                    for fc in range(KC):
                        last = nc.tensor.transpose(bank[0][:, oc * D + fc * P:oc * D + (fc + 1) * P],
                                                   wg_sb[:, (L * KC + fc) * D + oc * P:(L * KC + fc) * D + (oc + 1) * P], ident[:])
                last.then_inc(setup_mm, 1)
                pe.wait_ge(setup_dve, 2 + 3 * L)
                for fc in range(KC):
                    for j in range(2):
                        for oc in range(KC):
                            last = mm(bank[1][:, 2 * fc + j:2 * fc + j + 1], wgT[:, oc * D + fc * P:oc * D + (fc + 1) * P],
                                      a_cols[:, L * 4 + 2 * j + oc:L * 4 + 2 * j + oc + 1], start=oc == 0, stop=oc == KC - 1)
                last.then_inc(setup_mm, 1)
                pe.wait_ge(setup_dve, 3 + 3 * L)
                for fc in range(KC):
                    last = mm(bank[2][:, 0:2], ones32[:], u_cols[:, 2 * fc:2 * fc + 2], start=fc == 0, stop=fc == KC - 1)
                last.then_inc(setup_mm, 1)

            def scores_of(L, g):
                loop_wait(pe, diag_ready[L], at(g + 1))
                loop_wait(pe, E_ev[L], at(g))
                mm(bank[0][:], same_graph[:], diag[:], start=True, stop=False)
                mm(bank[0][:].rearrange("p (t j) -> p t j", t=GT), ident[:], bc(one("s1", g * GT, GT), NODES),
                   start=False, stop=True).then_inc(E_mm[L], 1)

            def turn_probs(L, g):
                loop_wait(pe, exp_done[L], at(g + 1))
                for h in range(2):
                    loop_wait(pe, PT_ev[L], at(2 * g + h - 1))
                    for j in range(4):
                        last = nc.tensor.transpose(bank[1 + h][:, j * P:(j + 1) * P],
                                                   probs[:, (4 * h + j) * P:(4 * h + j + 1) * P], ident[:])
                    last.then_inc(PT_mm[L], 1)

            def attend(L, g, more):
                def aggregate(q):
                    if q == 0:
                        loop_wait(pe, xn_ready[L], at(g + 1))
                    if q == 2:
                        loop_wait(pe, xn_half[L], at(g + 1))
                    if q % 2 == 0:
                        loop_wait(pe, PT_ev[L], at(2 * g + q // 2 + 1))
                    loop_wait(pe, G_ev[L], at(4 * g + q - 1))
                    for a in range(2):
                        for c in range(KC):
                            j = 2 * q + a
                            last = mm(bank[3 + q % 2][:, (2 * a + c) * P:(2 * a + c + 1) * P],
                                      xn[:, j * D + c * P:j * D + (c + 1) * P], probsT[:, j * P:(j + 1) * P],
                                      start=True, stop=True)
                    last.then_inc(G_mm[L], 1)

                def project(q):
                    loop_wait(pe, G_ev[L], at(4 * g + q + 1))
                    loop_wait(pe, ER_done[L], at(4 * g + q - 1))
                    for a in range(2):
                        for c in range(KC):
                            o = (q % 2) * 2 * D + a * D + c * P
                            last = mm(bank[5 + q % 2][:, a * D:(a + 1) * D], gT[:, o:o + P],
                                      wg_sb[:, (L * KC + c) * D:(L * KC + c + 1) * D], start=c == 0, stop=c == KC - 1)
                    last.then_inc(H_mm[L], 1)

                aggregate(0)
                if more:
                    scores_of(L, g + 1)
                aggregate(1)
                project(0)
                aggregate(2)
                project(1)
                aggregate(3)
                if more:
                    turn_probs(L, g + 1)
                project(2)
                project(3)

            for L in range(2):
                F = HID[L]
                FC = F // P
                edge_vectors(L)
                if L == 0:
                    for j in range(2):
                        for c in range(KC):
                            last = mm(bank[3][:, j * D + c * P:j * D + (c + 1) * P],
                                      u_cols[:, 2 * c + j:2 * c + j + 1].to_broadcast([P, P]), ident[:], start=True, stop=True)
                    last.then_inc(u_mm, 1)
                pe.wait_ge(setup_dve, 4 + 3 * L)
                def turn_x(i, q):
                    p = i * 4 + q
                    pe.wait_ge(x_copied[L], at(p + 1))
                    loop_wait(pe, xT_ev[L], at(p - 1))
                    for j in range(4):
                        last = nc.tensor.transpose(bank[q % 2][:, j * P:(j + 1) * P],
                                                   x_now[:, (4 * q + j) * P:(4 * q + j + 1) * P], ident[:])
                    last.then_inc(xT_mm[L], 1)

                def edge_dots(i, q):
                    p = i * 4 + q - 1
                    loop_wait(pe, xT_ev[L], at(p + 1))
                    for a in range(2):
                        for c in range(KC):
                            b = ((q - 1) % 2) * 2 * D + (2 * a + c) * P
                            last = mm(cut(bank[7], (2 * p + a) * 2, 2), xT[:, b:b + P],
                                      u_cols[:, c * 2:(c + 1) * 2], start=c == 0, stop=c == KC - 1)
                    last.then_inc(dot_mm[L], 1)

                for q in range(4):
                    turn_x(0, q)
                    if q:
                        edge_dots(0, q)
                with pe.Fori(1, X_TURNS[L]) as i:
                    for q in range(4):
                        turn_x(i, q)
                        edge_dots(i, q)
                edge_dots(X_TURNS[L], 0)
                pe.wait_ge(xT_ev[L], at(4 * X_TURNS[L]))
                scores_of(L, 0)
                turn_probs(L, 0)
                with pe.Fori(0, GROUPS - 1) as g:
                    attend(L, g, True)
                attend(L, GROUPS - 1, False)

                pe.wait_ge(setup_dve, 1)

                def turn_tokens(i, q):
                    pe.wait_ge(yl_ready[L], at(i * 8 + q + 1))
                    loop_wait(pe, yT_ev[L], at(i * 8 + q - 1))
                    for j in range(8):
                        last = nc.tensor.transpose(bank[q % 2][:, j * (P // 2):(j + 1) * (P // 2)].bitcast(F16),
                                                   y16[:, (8 * q + j) * P:(8 * q + j + 1) * P], ident16[:])
                    last.then_inc(yT_mm[L], 1)

                def logits(i, q):
                    p = i * 8 + q - 1
                    loop_wait(pe, yT_ev[L], at(p + 1))
                    for a in range(2):
                        for yh, kc in ((0, 0), (1, 0), (1, 1), (0, 1)):
                            n = E if yh else 2 * E
                            b = ((q - 1) % 2 * 8 + 4 * a + yh * KC + kc) * P
                            last = mm(cut(bank[6 + a], p * 2 * E, n), yT[:, b:b + P],
                                      rt16[:, (L * KC + kc) * 2 * E:(L * KC + kc) * 2 * E + n],
                                      start=(yh, kc) == (0, 0), stop=(yh, kc) == (0, 1))
                    last.then_inc(logit_mm[L], 1)

                for q in range(8):
                    turn_tokens(0, q)
                    if q:
                        logits(0, q)
                with pe.Fori(1, TILES // 16) as i:
                    for q in range(8):
                        turn_tokens(i, q)
                        logits(i, q)
                logits(TILES // 16, 0)
                pe.wait_ge(yT_ev[L], at(TILES // 2))

                pe.wait_ge(msum_ready[L], at(1))
                mm(bank[0][:], before16[:], msum[:, 0:512], start=True, stop=True)
                mm(bank[1][:], ones16[:], msum[:, 0:512], start=True, stop=True).then_inc(rank_mm[L], 1)
                pe.wait_ge(ab_ready[L], at(1))
                inv = bank[2][:, 0:STILES]
                mm(inv, inv_a[:, 0:P], inv_b[:, 0:STILES], start=True, stop=False).then_inc(inv_mm[L], 1)
                with pe.Fori(0, TILES // 4) as i:
                    for b in range(8):
                        if b % 4 == 0:
                            pe.wait_ge(onehot_ready[L], at(2 * i + b // 4 + 1))
                        pe.wait_ge(ab_ready[L], at(8 * i + b + 2))
                        mm(inv, inv_a[:, b * P:(b + 1) * P], inv_b[:, b * STILES:(b + 1) * STILES],
                           start=False, stop=False).then_inc(inv_mm[L], 1)
                pe.wait_ge(ab_ready[L], at(2 * TILES + 2))
                mm(inv, inv_a[:, 0:P], inv_b[:, 0:STILES], start=False, stop=True).then_inc(inv_mm[L], 1)

                def turn_over(i, s, u):
                    pe.wait_ge(gathered[u % SU], 16 * ST * (TURNS * L + i + u // SU + 1))
                    for j in range(4):
                        for a in range(ST):
                            q = (u % SU) * ST + a
                            last = nc.tensor.transpose(bank[u % 2][:, (j * ST + a) * (P // 2):(j * ST + a + 1) * (P // 2)].bitcast(F16),
                                                       gat[:, q * 512 + j * P:q * 512 + (j + 1) * P], ident16[:])
                    last.then_inc(T_mm[L], 1)

                def hidden(s, u, e):
                    loop_wait(pe, T_ev[L], at(s + 1))
                    for fc in range(FC):
                        n = 0
                        hb = bank[2 + 2 * (u % 2) + fc // 2][:, (fc % 2) * SLOT:(fc % 2 + 1) * SLOT]
                        for kc in range(KC):
                            for wh, yh in ((0, 0), (0, 1), (1, 0)):
                                tb = ((u % 2) * 4 + yh * KC + kc) * SLOT
                                last = mm(hb, w1_at(L, e, wh, kc, fc), tT[:, tb:tb + SLOT], start=n == 0, stop=n == 3 * KC - 1)
                                n += 1
                    last.then_inc(h_mm[L], 1)

                def output(s, u, e):
                    pe.wait_ge(h_split[L], at(s + 1))
                    loop_wait(pe, o_ev[L], at(s - 1))
                    ob = [bank[6 + u % 2][:, a * D:(a + 1) * D] for a in range(ST)]
                    hb = (u % 2) * 4 * SLOT
                    for a in range(ST):
                        for fc in range(FC):
                            for n, (hsrc, wh) in enumerate(((hid_hi, 0), (hid_lo, 0), (hid_hi, 1))):
                                h0 = hb + fc * SLOT + a * P
                                last = mm(ob[a], hsrc[:, h0:h0 + P], w2_at(L, e, wh, fc), start=fc == 0 and n == 0,
                                          stop=fc == FC - 1 and n == 2)
                    last.then_inc(o_mm[L], 1)

                def experts(i, more):
                    es = of_slots(pe, slot_block, i, SU + (2 if more else 0), 8 * F)
                    for u in range(SU):
                        s = i * SU + u
                        output(s, u, es[u])
                        if more or u + 3 < SU:
                            turn_over(i, s + 3, u + 3)
                        if more or u + 2 < SU:
                            hidden(s + 2, u + 2, es[u + 2])

                pe.wait_ge(slots_ready[L], at(1))
                first = of_slots(pe, slot_block, 0, 2, 8 * F)
                for s in range(2):
                    turn_over(0, s, s)
                hidden(0, 0, first[0])
                turn_over(0, 2, 2)
                hidden(1, 1, first[1])
                with pe.Fori(0, TURNS - 1) as i:
                    experts(i, True)
                experts(TURNS - 1, False)

        @block.scalar
        def _(act):
            credit(act, by_act)
            A = nc.scalar.activation

            def copy_scores(L, g):
                loop_wait(act, E_mm[L], at(g + 1))
                loop_wait(act, exp_done[L], at(g))
                A(scores, bank[0][:], ACT.Copy).then_inc(E_ev[L], 1)

            def exponent(L, g):
                loop_wait(act, sm_ready[L], at(g + 1))
                loop_wait(act, PT_mm[L], at(2 * g))
                loop_wait(act, rinv_ready[L], at(g))
                for r in range(2):
                    pr = slice(r * NODES, (r + 1) * NODES)
                    ins = A(probs.rearrange("p (t c) -> p t c", t=GT)[pr, :, r * NODES:(r + 1) * NODES],
                            scores.rearrange("p (t j) -> p t j", t=GT)[pr, :, :], ACT.Exp)
                ins.then_inc(exp_done[L], 1)

            def tokens_of(L, g):
                loop_wait(act, G_mm[L], at(4 * g))
                for j in range(GT // 2, GT):
                    t = g * GT + j
                    ins = A(xn[:, j * D:(j + 1) * D], xs(t), ACT.Identity, scale=one("rstd", t), bias=one("nmr", t))
                ins.then_inc(xn_half[L], 1)

            def copy_probs(L, g):
                for h in range(2):
                    loop_wait(act, PT_mm[L], at(2 * g + h + 1))
                    loop_wait(act, G_mm[L], at(4 * g + 2 * h - 2))
                    A(probsT[:, h * 512:(h + 1) * 512], bank[1 + h][:], ACT.Copy).then_inc(PT_ev[L], 1)

            def attend(L, g, more):
                def copy_g(q):
                    loop_wait(act, G_mm[L], at(4 * g + q + 1))
                    loop_wait(act, H_mm[L], at(4 * g + q - 1))
                    A(gT[:, (q % 2) * 512:(q % 2 + 1) * 512], bank[3 + q % 2][:], ACT.Copy).then_inc(G_ev[L], 1)

                def elu_parts(q):
                    loop_wait(act, H_mm[L], at(4 * g + q + 1))
                    if q == 0:
                        loop_wait(act, rinv_ready[L], at(g + 1))
                    loop_wait(act, post[L], at(4 * g + q - 1))
                    for a in range(2):
                        j = 2 * q + a
                        src = bank[5 + q % 2][:, a * D:(a + 1) * D]
                        b = (j % 4) * D
                        A(er_e[:, b:b + D], src, ACT.Exp, scale=rinv[:, j:j + 1])
                        ins = A(er_r[:, b:b + D], src, ACT.Relu, scale=rinv[:, j:j + 1])
                    ins.then_inc(ER_done[L], 1)

                if more:
                    copy_scores(L, g + 1)
                copy_g(0)
                copy_g(1)
                elu_parts(0)
                if more:
                    exponent(L, g + 1)
                copy_g(2)
                elu_parts(1)
                copy_g(3)
                if more:
                    copy_probs(L, g + 1)
                elu_parts(2)
                if more:
                    tokens_of(L, g + 1)
                elu_parts(3)

            for L in range(2):
                F = HID[L]
                FC = F // P
                def copy_x(i, q, more):
                    p = i * 4 + q
                    if more:
                        if L == 0:
                            loop_wait(act, x_loaded[q // 2 * 2], i * 16 + 16)
                            t = i * 16 + q // 2 * 8 + q % 2 * 2
                        else:
                            loop_wait(act, combined[0], at(2 * p + 2))
                            t = 2 * p
                        loop_wait(act, xT_mm[L], at(p - 3))
                        A(x_now[:, 2 * q * D:2 * (q + 1) * D], xs(t, 2), ACT.Copy).then_inc(x_copied[L], 1)
                    if not isinstance(p, int) or p:
                        loop_wait(act, xT_mm[L], at(p))
                        loop_wait(act, dot_mm[L], at(p - 2))
                        A(xT[:, ((q - 1) % 2) * 512:((q - 1) % 2 + 1) * 512], bank[(q - 1) % 2][:], ACT.Copy).then_inc(xT_ev[L], 1)

                for q in range(4):
                    copy_x(0, q, True)
                with act.Fori(1, X_TURNS[L]) as i:
                    for q in range(4):
                        copy_x(i, q, True)
                copy_x(X_TURNS[L], 0, False)
                act.wait_ge(var_ready[L], at(1))
                A(col["sd"], col["var"], ACT.Sqrt, bias=eps_col[:]).then_inc(sd_ready[L], 1)
                copy_scores(L, 0)
                act.wait_ge(s_ready[L], at(1))
                tokens_of(L, 0)
                exponent(L, 0)
                copy_probs(L, 0)
                with act.Fori(0, GROUPS - 1) as g:
                    attend(L, g, True)
                attend(L, GROUPS - 1, False)
                act.wait_ge(var_ready[L], at(2))
                A(col["sd"], col["var"], ACT.Sqrt, bias=eps_col[:]).then_inc(sd_ready[L], 1)
                act.wait_ge(rs2_ready[L], at(1))

                def normalise(i, q):
                    p = i * 4 + q
                    loop_wait(act, yl_ready[L], at(p - 3))
                    if L == 0:
                        loop_wait(act, x_plus_y[L], at(p - 3))
                    for a in range(2):
                        t = 2 * p + a
                        b = (2 * q + a) * D
                        ins = A(y32[:, b:b + D], xs(t), ACT.Identity, scale=one("rs2", t), bias=one("nm2", t))
                    ins.then_inc(y_ready[L], 1)

                with act.Fori(0, TILES // 8) as i:
                    for q in range(4):
                        normalise(i, q)
                with act.Fori(E // 2, E) as e:
                    for k in range(2):
                        stage, hi, _ = weight_parts(L, e, k)
                        loop_wait(act, weights_loaded[k][L], e * 16 + 16)
                        A(hi, stage, ACT.Copy, scale=WSCALE)
                        A(stage, stage, ACT.Copy, scale=WSCALE).then_inc(high_ready[L], 1)
                act.wait_ge(gap_ready[L], at(1))
                A(col["ta"], col["tb"], ACT.Exp).then_inc(e2_ready[L], 1)
                act.wait_ge(inv_mm[L], at(1))
                with act.Fori(0, TILES // 4) as i:
                    for k in range(TOPK):
                        part = slice(4 * k * P, 4 * (k + 1) * P)
                        loop_wait(act, diff_ready[L], at(2 * i + k + 1))
                        A(inv_d[:, part], inv_d[:, part], ACT.Abs).then_inc(abs_ready[L], 1)
                        loop_wait(act, abs_ready[L], at(2 * i + k + 1))
                        loop_wait(act, inv_mm[L], at(8 * i + 4 * k - 3))
                        A(inv_a[:, part], inv_d[:, part], ACT.Relu, scale=-1.0, bias=ones32[:, 0:1]).then_inc(onehot_ready[L], 1)

                def activate(s, u, e):
                    loop_wait(act, h_mm[L], at(s + 1))
                    loop_wait(act, h_split[L], at(s - 1))
                    base = L * E * HID[0] // P
                    for fc in range(FC):
                        h0 = ((u % 2) * 4 + fc) * SLOT
                        ins = A(hid[:, h0:h0 + SLOT], bank[2 + 2 * (u % 2) + fc // 2][:, (fc % 2) * SLOT:(fc % 2 + 1) * SLOT],
                                ACT.Gelu if L == 0 else ACT.Relu, bias=cut(b1T, e * FC + (base + fc), 1), scale=1.0 / WSCALE)
                    ins.then_inc(h_act[L], 1)

                def experts(i, more):
                    es = of_slots(act, slot_expert, i, SU + (2 if more else 0), 1)
                    for u in range(SU):
                        if more or u + 2 < SU:
                            activate(i * SU + u + 2, u + 2, es[u + 2])

                act.wait_ge(slots_ready[L], at(1))
                first = of_slots(act, slot_expert, 0, 2, 1)
                for s in range(2):
                    activate(s, s, first[s])
                with act.Fori(0, TURNS - 1) as i:
                    experts(i, True)
                experts(TURNS - 1, False)

        @block.vector
        def _(dve):
            credit(dve, by_dve)
            V = nc.vector
            ch = Chain(dve, own)
            tt, stt, ts = V.tensor_tensor, V.scalar_tensor_tensor, V.tensor_scalar
            stats3 = stats[:].rearrange("p (t s) -> p t s", s=6)

            def st(k):
                return stats3[:, :, k:k + 1].rearrange("p t one -> p (t one)")

            dve.wait_ge(const_ready, 1)
            dve.wait_ge(small_in, 16 * 10)
            dve.wait_ge(setup_mm, 1)
            ch.mark(V.tensor_copy(rt_sb[:, 0:KC * E], bank[2][:, 0:KC * E]))
            ch.wait()
            ch.mark(ts(rt_sb[:], rt_sb[:], WSCALE, None, ALU.mult))
            ch.wait()
            rt3 = rt_sb[:].rearrange("p (c e) -> p c e", e=E)
            rt16_3 = rt16[:].rearrange("p (c e) -> p c e", e=2 * E)
            ch.mark(V.tensor_copy(rt16_3[:, :, 0:E], rt3))
            ch.wait()
            tt(rt16_3[:, :, E:2 * E], rt3, rt16_3[:, :, 0:E], ALU.subtract).then_inc(setup_dve, 1)

            def mean_var(L):
                ch.mark(tt(col["ta"], st(1), st(4), ALU.add))
                ch.mark(tt(col["tb"], st(1), st(4), ALU.subtract))
                ch.mark(tt(col["tc"], st(2), st(5), ALU.add))
                ch.wait()
                ch.mark(ts(col["mean"], col["ta"], 0.5, None, ALU.mult))
                ch.mark(stt(col["td"], col["tb"], 0.25, col["tb"], ALU.mult, ALU.mult))
                ch.wait()
                stt(col["var"], col["tc"], 1.0 / D, col["td"], ALU.mult, ALU.add).then_inc(var_ready[L], 1)

            def rstd_of(L, n, r, m):
                dve.wait_ge(sd_ready[L], at(n))
                ch.mark(V.reciprocal(col[r], col["sd"]))
                ch.wait()
                ch.mark(stt(col[m], col["mean"], -1.0, col[r], ALU.mult, ALU.mult))
                ch.wait()

            def soft(L, g):
                loop_wait(dve, E_ev[L], at(g + 1))
                loop_wait(dve, neg_ready[L], at(g + 1))
                if L == 1:
                    ch.mark(stt(scores, scores, LEAK, scores, ALU.mult, ALU.max))
                    ch.wait()
                ch.mark(tt(scores, scores, neg, ALU.add))
                ch.wait()
                s3 = scores.rearrange("p (t j) -> p t j", t=GT)
                ch.mark(V.tensor_reduce(row_max, s3, AX.X, ALU.max))
                ch.wait()
                tt(s3, s3, bc(row_max, NODES), ALU.subtract).then_inc(sm_ready[L], 1)

            def tokens_of(L, g):
                loop_wait(dve, G_mm[L], at(4 * g - 2))
                for j in range(GT // 2):
                    ins = ts(xn[:, j * D:(j + 1) * D], xs(g * GT + j), one("rstd", g * GT + j), one("nmr", g * GT + j), ALU.mult, ALU.add)
                ins.then_inc(xn_ready[L], 1)

            def sums(L, g):
                loop_wait(dve, exp_done[L], at(g + 1))
                ch.mark(V.tensor_reduce(row_sum, probs.rearrange("p (t j) -> p t j", t=GT), AX.X, ALU.add))

            def attend(L, g, more):
                ch.wait()
                V.reciprocal(rinv, row_sum).then_inc(rinv_ready[L], 1)
                if more:
                    soft(L, g + 1)
                halves = {}
                for q in range(GT // 2 + 2):
                    if q < GT // 2:
                        b = (q % 2) * 2 * D
                        loop_wait(dve, ER_done[L], at(4 * g + q + 1))
                        halves[q] = ch.mark(stt(er_e[:, b:b + 2 * D], er_e[:, b:b + 2 * D], 1.0, er_r[:, b:b + 2 * D], ALU.min, ALU.add))
                    if 1 <= q <= GT // 2:
                        b = ((q - 1) % 2) * 2 * D
                        t = g * GT + 2 * (q - 1)
                        ch.wait(halves[q - 1])
                        stt(xs(t, 2), er_e[:, b:b + 2 * D], -1.0, xs(t, 2), ALU.add, ALU.add).then_inc(post[L], 1)
                    if 2 <= q:
                        loop_wait(dve, post[L], at(4 * g + q - 1))
                        for a in range(2):
                            t = g * GT + 2 * (q - 2) + a
                            ch.mark(V.bn_stats(cut(stats, t * 6, 6), xs(t)))
                    if q == 1 and more:
                        tokens_of(L, g + 1)
                    if q == 2 and more:
                        sums(L, g + 1)

            PER_ATTEND = 2 + GT // 2 + GT + 1
            for L in range(2):
                F = HID[L]
                FC = F // P
                dve.wait_ge(setup_mm, 2 + 3 * L)
                V.tensor_copy(wgT[:], bank[0][:]).then_inc(setup_dve, 1)
                dve.wait_ge(setup_mm, 3 + 3 * L)
                V.tensor_copy(u_cols[:], bank[1][:, 0:2 * KC]).then_inc(setup_dve, 1)
                dve.wait_ge(setup_mm, 4 + 3 * L)
                V.tensor_copy(u_sum[:], bank[2][:, 0:2]).then_inc(setup_dve, 1)

                if L == 0:
                    dve.wait_ge(u_mm, 1)
                    ch.mark(V.tensor_copy(u_rows, bank[3][:]))
                    with dve.Fori(0, TILES // 16) as i:
                        ch.enter(i, 16 + 16)
                        for c in range(4):
                            loop_wait(dve, x_loaded[c], i * 16 + 16)
                            for v in range(4):
                                t = i * 16 + 4 * c + v
                                ch.mark(V.bn_stats(cut(stats, t * 6, 6), xs(t)))
                            if c % 2:
                                ch.wait(ch.n - 4)
                                for v in range(8):
                                    ch.mark(stt(junk[:, v * D:(v + 1) * D], xs(i * 16 + 4 * c + v // 2), 1.0,
                                                u_rows[:, (v % 2) * D:(v % 2 + 1) * D], ALU.mult, ALU.mult,
                                                accum_out=cut(dots, (i * 16 + 4 * c) * 2 + v, 1)))
                    ch.leave(TILES // 16)
                else:
                    combine(dve, ch, 0, True)
                ch.wait()
                mean_var(L)
                rstd_of(L, 1, "rstd", "nmr")
                dve.wait_ge(dot_mm[L], at(4 * X_TURNS[L]))
                dve.wait_ge(setup_dve, 4 + 3 * L)
                if L == 0:
                    ch.mark(V.tensor_copy(dots.rearrange("p (c two x) -> p c two x", two=2, x=8)[:, :, 0, :],
                                          bank[7][:, 0:TILES].rearrange("p (c x) -> p c x", x=8)))
                else:
                    ch.mark(V.tensor_copy(dots, bank[7][:, 0:2 * TILES]))
                ch.wait()
                for j in range(2):
                    dot = dots.rearrange("p (t j) -> p t j", j=2)[:, :, j:j + 1].rearrange("p t one -> p (t one)")
                    ch.mark(tt(col["ta"], dot, col["rstd"], ALU.mult))
                    ch.wait()
                    ins = stt(col[f"s{j + 1}"], col["nmr"], u_sum[:, j:j + 1], col["ta"], ALU.mult, ALU.add)
                    if j == 0:
                        ch.mark(ins)
                        ch.wait()
                    else:
                        ins.then_inc(s_ready[L], 1)

                ch.mark(V.memset(probs, 0.0))
                soft(L, 0)
                tokens_of(L, 0)
                sums(L, 0)
                with dve.Fori(0, GROUPS - 1) as g:
                    ch.enter(g, PER_ATTEND + L)
                    attend(L, g, True)
                ch.leave(GROUPS - 1)
                attend(L, GROUPS - 1, False)

                ch.wait()
                mean_var(L)
                rstd_of(L, 2, "rs2", "nm2")
                V.memset(ex[:], 0.0).then_inc(rs2_ready[L], 1)
                y16_4 = y16.rearrange("p (t c) -> p t c", c=2 * D)
                y32_4 = y32.rearrange("p (t d) -> p t d", d=D)

                def cut_tokens(i, q, first):
                    p = i * 8 + q
                    w, v = (q - 1) % 8, (q - 2) % 2
                    if not (isinstance(p, int) and p >= TILES // 2):
                        if q % 2 == 0:
                            loop_wait(dve, y_stored[q // 2][L], 16 + i * 16)
                        loop_wait(dve, yT_mm[L], at(p - 7))
                        loop_wait(dve, y_ready[L], at(p + 1))
                        V.tensor_copy(y16_4[:, 2 * q:2 * q + 2, 0:D], y32_4[:, 2 * (q % 4):2 * (q % 4) + 2, :]).then_inc(hi_ready[L], 1)
                    if not (first and q < 1) and not (isinstance(p, int) and p > TILES // 2):
                        loop_wait(dve, hi_ready[L], at(p))
                        tt(y16_4[:, 2 * w:2 * w + 2, D:2 * D], y32_4[:, 2 * (w % 4):2 * (w % 4) + 2, :],
                           y16_4[:, 2 * w:2 * w + 2, 0:D], ALU.subtract).then_inc(yl_ready[L], 1)
                    if not (first and q < 2):
                        loop_wait(dve, yT_mm[L], at(p - 1))
                        loop_wait(dve, logit_mm[L], at(p - 3))
                        V.tensor_copy(yT[:, v * 1024:(v + 1) * 1024], bank[v][:].bitcast(F16)).then_inc(yT_ev[L], 1)

                for q in range(8):
                    cut_tokens(0, q, True)
                with dve.Fori(1, TILES // 16) as i:
                    for q in range(8):
                        cut_tokens(i, q, False)
                for q in range(2):
                    cut_tokens(TILES // 16, q, False)

                dve.wait_ge(logit_mm[L], at(TILES // 2))
                dve.wait_ge(yl_ready[L], at(TILES // 2))
                dve.wait_ge(yT_ev[L], at(TILES // 2))
                if L == 0:
                    dve.wait_ge(x_plus_y[L], at(TILES // 2))
                for h in range(4):
                    dve.wait_ge(y_stored[h][L], 16 + 16 * (TILES // 16))
                te = lambda a: a.rearrange("p (t e) -> p t e", e=E)
                et = lambda a: a.rearrange("p (e t) -> p e t", e=E)
                by_pair = lambda a_, j: a_.rearrange("p (t x) -> p t x", x=2 * E)[:, :, j * E:(j + 1) * E]
                for a in range(2):
                    ch.mark(ts(by_pair(lg2, a), by_pair(bank[6 + a][:], 1), 1.0 / WSCALE, None, ALU.mult))
                ch.wait()
                for a in range(2):
                    ch.mark(stt(by_pair(lg, a), by_pair(bank[6 + a][:], 0), 1.0 / WSCALE, by_pair(lg2, a), ALU.mult, ALU.add))
                if L == 1:
                    ch.wait()
                    ch.mark(tt(te(lg), te(lg), rows(gb_bc[:, 0:E], TILES), ALU.add))
                    ch.wait()
                    ch.mark(tt(te(lg), te(lg), rows(gb_bc[:, E:2 * E], TILES), ALU.add))
                ch.wait()
                for src, mx, M in ((lg, "m1", M1), (lg2, "m2", M2)):
                    ch.mark(V.tensor_reduce(col[mx], te(src), AX.X, ALU.max))
                    ch.wait()
                    ch.mark(tt(te(eqm), te(src), bc(col[mx], E), ALU.is_equal))
                    ch.wait()
                    ch.mark(tt(te(sc), te(eqm), rows(rank8[:], TILES), ALU.mult))
                    ch.wait()
                    ch.mark(V.tensor_reduce(col["rk"], te(sc), AX.X, ALU.max))
                    ch.wait()
                    ch.mark(tt(te(M), te(sc), bc(col["rk"], E), ALU.is_equal))
                    ch.wait()
                    if M is M1:
                        ch.mark(stt(lg2, M1, -3.0e38, lg, ALU.mult, ALU.add))
                        ch.wait()
                tt(col["tb"], col["m2"], col["m1"], ALU.subtract).then_inc(gap_ready[L], 1)
                tt(msum[:, 0:512], M1, M2, ALU.add).then_inc(msum_ready[L], 1)
                ch.mark(V.memset(onesd, 1.0))
                dve.wait_ge(rank_mm[L], at(1))
                ch.mark(V.tensor_copy(et(big_a), bank[1][:].rearrange("p (t e) -> p e t", e=E)))
                ch.wait()
                ch.mark(V.tensor_tensor_scan(big_b, onesd, big_a, 0.0, ALU.mult, ALU.add))
                ch.wait()
                ends, cnt, nt, slots_to, base, adj_e = (ex[:, 9 * k:9 * k + 9] for k in range(6))
                ch.mark(V.memset(ex[:], 0.0))
                ch.wait()
                ch.mark(V.tensor_copy(ends[:, 1:9].rearrange("p (e one) -> p e one", one=1), et(big_b)[:, :, TILES - 1:TILES]))
                ch.wait()
                ch.mark(tt(cnt[:, 0:E], ends[:, 1:9], ends[:, 0:8], ALU.subtract))
                ch.wait()
                ch.mark(ts(ex_i[:, 0:E], cnt[:, 0:E], float(SLOT - 1), None, ALU.add))
                ch.wait()
                ch.mark(ts(ex_i[:, E:2 * E], ex_i[:, 0:E], SLOT.bit_length() - 1, None, ALU.arith_shift_right))
                ch.wait()
                ch.mark(V.tensor_copy(nt[:, 0:E], ex_i[:, E:2 * E]))
                ch.wait()
                ch.mark(V.tensor_tensor_scan(slots_to[:, 0:E], onesd[:, 0:E], nt[:, 0:E], 0.0, ALU.mult, ALU.add))
                ch.wait()
                ch.mark(tt(base[:, 0:E], slots_to[:, 0:E], nt[:, 0:E], ALU.subtract))
                ch.wait()
                ch.mark(stt(adj_e[:, 0:E], base[:, 0:E], float(SLOT), ends[:, 0:8], ALU.mult, ALU.subtract))
                ch.mark(tt(big_b, big_b, big_a, ALU.subtract))
                ch.wait()
                ch.mark(tt(et(big_b), et(big_b), bc(adj_e[:, 0:E], TILES), ALU.add))
                ch.wait()
                ch.mark(tt(pf.rearrange("p (t e) -> p e t", e=E), et(big_b), bank[0][:].rearrange("p (t e) -> p e t", e=E), ALU.add))
                ch.wait()
                for k, M in enumerate((M1, M2)):
                    ch.mark(tt(big_a, M, pf, ALU.mult))
                    ch.wait()
                    ch.mark(V.tensor_reduce(col["rk"], te(big_a), AX.X, ALU.add))
                    ch.wait()
                    ch.mark(V.tensor_copy(pos_i[k][:], col["rk"]))
                    ch.wait()
                    ch.mark(ts(tmp_i[:], pos_i[k][:], P - 1, None, ALU.bitwise_and))
                    ch.wait()
                    ch.mark(V.tensor_copy(col[f"lo{k}"], tmp_i[:]))
                    ch.wait()
                    ch.mark(ts(tmp_i[:], pos_i[k][:], 7, None, ALU.arith_shift_right))
                    ch.wait()
                    ch.mark(V.tensor_copy(col[f"hi{k}"], tmp_i[:]))
                    ch.wait()
                ch.mark(V.memset(inv_a[:, 0:P], 0.0))
                ch.wait()
                V.memset(inv_b[:, 0:STILES], 0.0).then_inc(ab_ready[L], 1)
                dve.wait_ge(inv_mm[L], at(1))
                with dve.Fori(0, TILES // 4) as i:
                    for k in range(TOPK):
                        loop_wait(dve, inv_mm[L], at(8 * i + 4 * k - 3))
                        for v in range(4):
                            b, t = 4 * k + v, 4 * i + v
                            ts(inv_b[:, b * STILES:(b + 1) * STILES], iota_s[:], one(f"hi{k}", t), cut(row_id, TILES * k + t, 1),
                               ALU.is_equal, ALU.mult).then_inc(ab_ready[L], 1)
                dve.wait_ge(inv_mm[L], at(2 * TILES + 1))
                ch.mark(V.memset(inv_a[:, 0:P], 0.0))
                ch.wait()
                V.memset(inv_b[:, 0:STILES], 0.0).then_inc(ab_ready[L], 1)
                ct = cmp_t[0:1, :].rearrange("p (s e) -> p s e", e=E)
                ch.mark(tt(ct, slots_to[0:1, 0:E].rearrange("p (one e) -> p one e", one=1).to_broadcast([1, SLOTS, E]),
                           iota_s[0:1, 0:SLOTS].rearrange("p (s one) -> p s one", one=1).to_broadcast([1, SLOTS, E]), ALU.is_le))
                ch.wait()
                ch.mark(V.tensor_reduce(big_a[0:1, 0:SLOTS], ct, AX.X, ALU.add))
                ch.wait()
                ch.mark(ts(slot_expert[:, 0:SLOTS], big_a[0:1, 0:SLOTS], float(E - 1), None, ALU.min))
                ch.mark(ts(slot_block[:, 0:SLOTS], big_a[0:1, 0:SLOTS], float(E - 1), float(8 * F), ALU.min, ALU.mult))
                dve.wait_ge(e2_ready[L], at(1))
                ch.mark(ts(col["tc"], col["ta"], 1.0, None, ALU.add))
                ch.wait()
                ch.mark(V.reciprocal(col["w1"], col["tc"]))
                ch.wait()
                ch.mark(tt(col["w2"], col["ta"], col["w1"], ALU.mult))
                ch.wait()
                dve.wait_ge(inv_mm[L], at(2 * TILES + 2))
                ch.mark(V.tensor_copy(inv_v, bank[2][:, 0:STILES]))
                ch.wait()
                ch.mark(ts(inv_i, inv_v, -1.0, None, ALU.add))
                ch.mark(stt(inv_x, inv_v, 0.0, dump_id[:], ALU.is_equal, ALU.mult))
                ch.wait()
                ch.mark(stt(scatter_row[:], inv_v, -1.0, inv_x, ALU.add, ALU.add))
                ch.wait()
                ts(gather_row[:].bitcast(I32), inv_i, TOKENS - 1, None, ALU.bitwise_and).then_inc(slots_ready[L], 1)

                def copy_T(s, u):
                    loop_wait(dve, T_mm[L], at(s + 1))
                    loop_wait(dve, h_mm[L], at(s - 1))
                    V.tensor_copy(tT[:, (u % 2) * 4 * SLOT:(u % 2 + 1) * 4 * SLOT], bank[u % 2][:].bitcast(F16)).then_inc(T_ev[L], 1)

                def cut_hidden(s, u):
                    loop_wait(dve, h_act[L], at(s + 1))
                    loop_wait(dve, o_mm[L], at(s - 1))
                    hb = (u % 2) * 4 * SLOT
                    ch.mark(V.tensor_copy(hid_hi[:, hb:hb + FC * SLOT], hid[:, hb:hb + FC * SLOT]))
                    ch.wait()
                    tt(hid_lo[:, hb:hb + FC * SLOT], hid[:, hb:hb + FC * SLOT], hid_hi[:, hb:hb + FC * SLOT], ALU.subtract).then_inc(h_split[L], 1)

                def copy_out(s, u, i, e):
                    loop_wait(dve, o_mm[L], at(s + 1))
                    if used_before(L, i):
                        for a in range(ST):
                            loop_wait(dve, scattered[u * ST + a], 16 * TURNS * L + 16 * i)
                    stt(o_sb[:, u * ST * D:(u + 1) * ST * D].rearrange("p (a d) -> p a d", a=ST),
                        bank[6 + u % 2][:, 0:ST * D].rearrange("p (a d) -> p a d", a=ST), 1.0 / WSCALE,
                        rows(cut(b2_bc, e * D, D), ST), ALU.mult, ALU.add).then_inc(o_ev[L], 1)

                def experts(i, more):
                    es = of_slots(dve, slot_expert, i, SU, 1)
                    for u in range(SU):
                        s = i * SU + u
                        if more or u + 1 < SU:
                            cut_hidden(s + 1, u + 1)
                        copy_out(s, u, i, es[u])
                        if more or u + 3 < SU:
                            copy_T(s + 3, u + 3)

                dve.wait_ge(b2_in, 16 * (L + 1))
                copy_T(0, 0)
                copy_T(1, 1)
                copy_T(2, 2)
                cut_hidden(0, 0)
                experts(0, True)
                with dve.Fori(1, TURNS - 1) as i:
                    ch.enter(i - 1, SU)
                    experts(i, True)
                ch.leave(TURNS - 2)
                experts(TURNS - 1, False)
            combine(dve, ch, 1, False)


_INS = ["x", "adj", "L0_gnn_W", "L0_gnn_a", "L0_ffn_router_w", "L0_ffn_w1", "L0_ffn_b1", "L0_ffn_w2", "L0_ffn_b2",
        "L1_gnn_W", "L1_gnn_a", "L1_ffn_Wg", "L1_ffn_bg", "L1_ffn_bias", "L1_ffn_W1", "L1_ffn_b1", "L1_ffn_W2", "L1_ffn_b2"]


def kernel(**inputs):
    import numpy as _np
    import concourse.bacc as _bacc
    from concourse import mybir as _mybir
    from concourse.bass_utils import run_bass_kernel_spmd as _run

    nc = _bacc.Bacc("TRN2", target_bir_lowering=False, num_devices=1)
    arrays, t = {}, {}
    for name in _INS:
        a = _np.ascontiguousarray(inputs[name])
        arrays[f"in_{name}"] = a
        t[name] = nc.dram_tensor(f"in_{name}", a.shape, _mybir.dt.from_np(a.dtype), kind="ExternalInput").ap()
    out = nc.dram_tensor("out_0", (GRAPHS, NODES, D), F32, kind="ExternalOutput").ap()
    build(nc, t["x"], t["adj"], (t["L0_gnn_W"], t["L1_gnn_W"]), (t["L0_gnn_a"], t["L1_gnn_a"]),
          (t["L0_ffn_router_w"], t["L1_ffn_Wg"]), t["L1_ffn_bg"], t["L1_ffn_bias"],
          (t["L0_ffn_w1"], t["L1_ffn_W1"]), (t["L0_ffn_b1"], t["L1_ffn_b1"]),
          (t["L0_ffn_w2"], t["L1_ffn_W2"]), (t["L0_ffn_b2"], t["L1_ffn_b2"]), out)
    r = _run(nc, [arrays], core_ids=[0])
    return r.results[0]["out_0"]
```
